# Optimizing a Trainium2 kernel written in Bass

```python
import numpy as np
import jax
import jax.numpy as jnp

def _softmax(x, axis=-1):
    return jax.nn.softmax(x, axis=axis)

def _gelu(x):
    return jax.nn.gelu(x, approximate=True)

def _silu(x):
    return jax.nn.silu(x)

def _sigmoid(x):
    return jax.nn.sigmoid(x)

def _layernorm(x, axis=-1, eps=1e-05):
    m = jnp.mean(x, axis=axis, keepdims=True)
    v = jnp.var(x, axis=axis, keepdims=True)
    return (x - m) / jnp.sqrt(v + eps)

def _scatter_add(tgt, idx, src, axis=0):
    return tgt.at[idx].add(src)

def _segment_sum(src, seg, n):
    return jax.ops.segment_sum(src, seg, n)
kernel_name = 'mk_gnn_preln_d2_gnn_r32_c376fd'

def setup_inputs(seed: int=0):
    np.random.seed(seed)
    _w = jnp.asarray

    def _rec_inputs():
        import jax
        import jax.numpy as jnp
        _gk = jax.random.key(seed)
        x = -0.000202 + 1 * jax.random.normal(jax.random.fold_in(_gk, 1), (50000, 128), jnp.float32)
        src = jax.random.randint(jax.random.fold_in(_gk, 2), (50000,), 0, 50000, jnp.int32)
        dst = jnp.minimum((50000 * jax.random.uniform(jax.random.fold_in(_gk, 3), (50000,)) ** 2.0).astype(jnp.int32), 49999)
        _o = jnp.argsort(dst, stable=True)
        src = src[_o]
        dst = dst[_o]
        edge_type_3 = jax.random.randint(jax.random.fold_in(_gk, 13), (50000,), 0, 3, jnp.int32)
        edge_type_8 = jax.random.randint(jax.random.fold_in(_gk, 14), (50000,), 0, 8, jnp.int32)
        return (x, src, dst, edge_type_3, edge_type_8)
    x, src, dst, edge_type_3, edge_type_8 = _rec_inputs()

    def _L0_gnn_setup():
        import jax, jax.numpy as jnp
        import numpy as np
        N_NODES = 50000
        N_EDGES = 9375
        INPUT_DIM = 128
        HIDDEN_DIM = 256
        NUM_HEADS = 8
        HEAD_DIM = HIDDEN_DIM // NUM_HEADS
        NUM_EDGE_TYPES = 3
        key = jax.random.key(seed)
        ks = jax.random.split(key, 12)
        s_in = 1.0 / np.sqrt(INPUT_DIM)
        s_hid = 1.0 / np.sqrt(HIDDEN_DIM)
        return {'node_features': jax.random.normal(ks[0], (N_NODES, INPUT_DIM), jnp.float32), 'edges': jax.random.randint(ks[1], (N_EDGES, 2), 0, N_NODES), 'edge_types': jax.random.randint(ks[2], (N_EDGES,), 0, NUM_EDGE_TYPES), 'Wq': jax.random.normal(ks[3], (HIDDEN_DIM, INPUT_DIM), jnp.float32) * s_in, 'bq': jax.random.normal(ks[4], (HIDDEN_DIM,), jnp.float32) * s_in, 'Wk': jax.random.normal(ks[5], (HIDDEN_DIM, INPUT_DIM), jnp.float32) * s_in, 'bk': jax.random.normal(ks[6], (HIDDEN_DIM,), jnp.float32) * s_in, 'Wv': jax.random.normal(ks[7], (HIDDEN_DIM, INPUT_DIM), jnp.float32) * s_in, 'bv': jax.random.normal(ks[8], (HIDDEN_DIM,), jnp.float32) * s_in, 'edge_emb': jax.random.normal(ks[9], (NUM_EDGE_TYPES, HIDDEN_DIM), jnp.float32), 'Wo': jax.random.normal(ks[10], (INPUT_DIM, HIDDEN_DIM), jnp.float32) * s_hid, 'bo': jax.random.normal(ks[11], (INPUT_DIM,), jnp.float32) * s_hid}
    _L0_gnn_all = _L0_gnn_setup()
    _L0_gnn_in = {k: v for k, v in _L0_gnn_all.items() if k in ('Wq', 'bq', 'Wk', 'bk', 'Wv', 'bv', 'edge_emb', 'Wo', 'bo')}
    del _L0_gnn_all

    def _L1_gnn_setup():
        import jax, jax.numpy as jnp
        import numpy as np
        IN_DIM = 128
        OUT_DIM = 128
        NUM_RELS = 8
        N_NODES = 50000
        N_EDGES = 15625
        key = jax.random.key(seed)
        k_x, k_ei_s, k_ei_d, k_et, k_w, k_sw = jax.random.split(key, 6)
        x = jax.random.normal(k_x, (N_NODES, IN_DIM), dtype=jnp.float32)
        src = jax.random.randint(k_ei_s, (N_EDGES,), 0, N_NODES)
        dst = jax.random.randint(k_ei_d, (N_EDGES,), 0, N_NODES)
        edge_index = jnp.stack([src, dst], axis=0).astype(jnp.int64)
        edge_type = jax.random.randint(k_et, (N_EDGES,), 0, NUM_RELS).astype(jnp.int64)
        bw = float(np.sqrt(6.0 / (IN_DIM + OUT_DIM)))
        weight = jax.random.uniform(k_w, (NUM_RELS, IN_DIM, OUT_DIM), dtype=jnp.float32, minval=-bw, maxval=bw)
        self_loop_weight = jax.random.uniform(k_sw, (IN_DIM, OUT_DIM), dtype=jnp.float32, minval=-bw, maxval=bw)
        bias = jnp.zeros((OUT_DIM,), dtype=jnp.float32)
        return {'x': x, 'weight': weight, 'self_loop_weight': self_loop_weight, 'bias': bias, 'edge_index': edge_index, 'edge_type': edge_type, 'num_entities': N_NODES}
    _L1_gnn_all = _L1_gnn_setup()
    _L1_gnn_in = {k: v for k, v in _L1_gnn_all.items() if k in ('weight', 'self_loop_weight', 'bias')}
    del _L1_gnn_all
    return {'x': x, 'src': src, 'dst': dst, 'edge_type_3': edge_type_3, 'edge_type_8': edge_type_8, 'L0_gnn_Wq': _L0_gnn_in['Wq'], 'L0_gnn_bq': _L0_gnn_in['bq'], 'L0_gnn_Wk': _L0_gnn_in['Wk'], 'L0_gnn_bk': _L0_gnn_in['bk'], 'L0_gnn_Wv': _L0_gnn_in['Wv'], 'L0_gnn_bv': _L0_gnn_in['bv'], 'L0_gnn_edge_emb': _L0_gnn_in['edge_emb'], 'L0_gnn_Wo': _L0_gnn_in['Wo'], 'L0_gnn_bo': _L0_gnn_in['bo'], 'L1_gnn_weight': _L1_gnn_in['weight'], 'L1_gnn_self_loop_weight': _L1_gnn_in['self_loop_weight'], 'L1_gnn_bias': _L1_gnn_in['bias']}

def reference(x, src, dst, edge_type_3, edge_type_8, L0_gnn_Wq, L0_gnn_bq, L0_gnn_Wk, L0_gnn_bk, L0_gnn_Wv, L0_gnn_bv, L0_gnn_edge_emb, L0_gnn_Wo, L0_gnn_bo, L1_gnn_weight, L1_gnn_self_loop_weight, L1_gnn_bias):
    import jax
    import jax.numpy as jnp

    def _L0_gnn_ref(node_features, edges, edge_types, Wq, bq, Wk, bk, Wv, bv, edge_emb, Wo, bo):
        import jax, jax.numpy as jnp
        import numpy as np
        N_NODES = 50000
        N_EDGES = 9375
        INPUT_DIM = 128
        HIDDEN_DIM = 256
        NUM_HEADS = 8
        HEAD_DIM = HIDDEN_DIM // NUM_HEADS
        NUM_EDGE_TYPES = 3
        Q = (node_features @ Wq.T + bq).reshape(-1, NUM_HEADS, HEAD_DIM)
        K = (node_features @ Wk.T + bk).reshape(-1, NUM_HEADS, HEAD_DIM)
        V = (node_features @ Wv.T + bv).reshape(-1, NUM_HEADS, HEAD_DIM)
        src = edges[:, 0]
        tgt = edges[:, 1]
        scale = 1.0 / jnp.sqrt(jnp.float32(HEAD_DIM))
        scores = jnp.einsum('ehd,egd->ehg', Q[src], K[tgt]) * scale
        attn = jax.nn.softmax(scores, axis=-1)
        msg = jnp.einsum('ehg,egd->ehd', attn, V[tgt]).reshape(-1, HIDDEN_DIM)
        msg = msg + edge_emb[edge_types]
        out_e = msg @ Wo.T + bo
        messages = jax.ops.segment_sum(out_e, src, num_segments=N_NODES)
        return messages

    def _L1_gnn_ref(x, weight, self_loop_weight, bias, edge_index, edge_type, num_entities):
        import jax, jax.numpy as jnp
        import numpy as np
        IN_DIM = 128
        OUT_DIM = 128
        NUM_RELS = 8
        N_NODES = 50000
        N_EDGES = 15625
        hr = jnp.einsum('nd,rdo->rno', x, weight)
        src, dst = (edge_index[0], edge_index[1])
        msg = hr[edge_type, src]
        agg = jax.ops.segment_sum(msg, dst, num_segments=num_entities)
        out = agg + x @ self_loop_weight + bias
        return jax.nn.relu(out)
    edge_index = jnp.stack([src, dst])
    edge_index_t = jnp.stack([src, dst], axis=1)
    h = jnp.maximum(_layernorm(x, axis=-1), 0.0)
    x = x + _L0_gnn_ref(h, edge_index_t, edge_type_3, L0_gnn_Wq, L0_gnn_bq, L0_gnn_Wk, L0_gnn_bk, L0_gnn_Wv, L0_gnn_bv, L0_gnn_edge_emb, L0_gnn_Wo, L0_gnn_bo)
    h = jnp.maximum(_layernorm(x, axis=-1), 0.0)
    x = x + _L1_gnn_ref(h, L1_gnn_weight, L1_gnn_self_loop_weight, L1_gnn_bias, edge_index, edge_type_8, 50000)
    return x

_drawn_inputs = setup_inputs


def setup_inputs(seed=0):
    import zlib

    import numpy as np

    out = dict(_drawn_inputs(seed))
    spreads = {'L1_gnn_bias': (0.0, 0.1)}
    factors = {'L0_gnn_bq': 5.627, 'L0_gnn_bk': 4.589}
    for name, (base, spread) in spreads.items():
        noise = np.random.default_rng([zlib.crc32(name.encode()), seed]).standard_normal(out[name].shape)
        drawn = base * np.exp(spread * noise) if base else spread * noise
        out[name] = jnp.asarray(drawn.astype(out[name].dtype))
    for name, factor in factors.items():
        out[name] = (out[name] * factor).astype(out[name].dtype)
    return out
```

```python
import concourse.bass as bass
from concourse import mybir
from contextlib import ExitStack

F32 = mybir.dt.float32
I32 = mybir.dt.int32
ALU = mybir.AluOpType
ACT = mybir.ActivationFunctionType
AX = mybir.AxisListType

P = 128
D = 128
H = 8
DH = 32
HID = H * DH
N = 50000
E = 50000
T3 = 3
R = 8
J = 4
NB = -(-E // (P * J))
COLS = NB * J
ROWS = NB * P * J
EG = 4
G = P // EG
TOK = EG * H
EPS = 1e-5
SCALE = float(DH) ** -0.5


def is_past(b, k):
    return not isinstance(b, int) or b >= k


def counts(eng, *values):
    return [v if isinstance(v, int) else eng.to_reg(v) for v in values]


def build(nc, x, src, dst, et3, et8, wqT, bqT, wkT, bkT, wvT, bvT, embT, woT, bo, wrel, wself, bias1, out):
    x1 = nc.dram_tensor("x1", (ROWS, D), F32, kind="Internal").ap()
    h2 = nc.dram_tensor("h2", (ROWS, D), F32, kind="Internal").ap()
    agg = nc.dram_tensor("agg", (ROWS, D), F32, kind="Internal").ap()

    ctx = ExitStack()
    with ctx:
        def sb(name, shape, dt=F32):
            return ctx.enter_context(nc.sbuf_tensor(name, shape, dt))

        def sem(name):
            return ctx.enter_context(nc.semaphore(name))

        ident = sb("ident", [P, P])
        lower = sb("lower", [P, P])
        col_less_row = sb("col_less_row", [P, P], I32)
        own_edge = sb("own_edge", [P, EG])
        edge_of_row = sb("edge_of_row", [P, EG], I32)
        edge_no = sb("edge_no", [P, EG], I32)
        rel_no = sb("rel_no", [P, R], I32)
        part_no = sb("part_no", [P, 1], I32)
        part_f = sb("part_f", [P, 1])
        minus_half = sb("minus_half", [P, 2 * J])
        zeros = sb("zeros", [P, D])
        wq = sb("wq", [P, HID])
        wk = sb("wk", [P, HID])
        wv = sb("wv", [P, HID])
        wo = sb("wo", [P, 2, D])
        emb = sb("emb", [P, 2, T3])
        bq = sb("bq", [P, H])
        bk = sb("bk", [P, H])
        bv = sb("bv", [P, H])
        bo3 = sb("bo3", [T3, D])
        type_out = sb("type_out", [T3, D])
        w_rel = sb("w_rel", [P, R, D])
        w_self = sb("w_self", [P, D])
        b_self = sb("b_self", [P, D])

        raw = sb("raw", [P, 4, COLS], I32)
        gather_idx = sb("gather_idx", [P, NB, 2 * J], I32)
        dump = sb("dump", [P, COLS], I32)
        src_tab = sb("src_tab", [P, NB, 3 * J])
        dst_tab = sb("dst_tab", [P, NB, 3 * J])

        g_idx = sb("g_idx", [P, 2 * J], I32)
        xg = sb("xg", [P, 2 * J, D])
        stats = sb("stats", [P, 2 * J, 6])
        mv = sb("mv", [P, 2 * J, 2])
        var_e = sb("var_e", [P, 2 * J])
        rstd = sb("rstd", [P, 2 * J])
        nbias = sb("nbias", [P, 2 * J])
        hg = sb("hg", [P, 2 * J, D])
        hTs = sb("hTs", [P, J * P])
        hTd = sb("hTd", [P, J * P])
        q_tok = sb("q_tok", [P, G * TOK])
        k_tok = sb("k_tok", [P, G * TOK])
        v_tok = sb("v_tok", [P, G * TOK])
        own_sc = sb("own_sc", [P, G * TOK])
        sc = sb("sc", [P, G, H])
        mx = sb("mx", [P, G])
        cen = sb("cen", [P, G, H])
        ex = sb("ex", [P, G, H])
        den = sb("den", [P, G])
        rden = sb("rden", [P, G])
        pr = sb("pr", [P, G, H])
        a_tok = sb("a_tok", [P, G * TOK])
        aT = sb("aT", [P, G * TOK])
        vT = sb("vT", [P, G * TOK])
        m_strip = sb("m_strip", [P, H, P])
        m_dense = sb("m_dense", [P, 2, J, P])
        edge_f = sb("edge_f", [P, 3 * J])
        same = sb("same", [P, J, P])
        earlier = sb("earlier", [P, J, P])
        count = sb("count", [P, J])
        moved = sb("moved", [P, J])
        s_key = sb("s_key", [P, 2 * J])
        s_idx = sb("s_idx", [P, J], I32)
        type_hot = sb("type_hot", [T3, J * P])
        out_e = sb("out_e", [P, J, D])
        summed = sb("summed", [P, J, D])

        def pb(name, shape):
            return ctx.enter_context(nc.psum_tensor(name, shape, F32))
        ps_a = pb("ps_a", [P, 1024])
        ps_b = pb("ps_b", [P, 1024])
        ps_c = pb("ps_c", [P, 1024])
        ps_d = pb("ps_d", [P, 512])
        ps_e = pb("ps_e", [P, 512])

        loaded = sem("loaded")
        pads_ready = sem("pads_ready")
        const_pool = sem("const_pool")
        const_ready = sem("const_ready")
        tables_ready = sem("tables_ready")
        type_ready = sem("type_ready")
        type_psum = sem("type_psum")
        x1_set = sem("x1_set")
        prep = sem("prep")

        block = ctx.enter_context(nc.Block())

        gidx_ready = sem("gidx_ready")
        gathered = sem("gathered")
        stats_done = sem("stats_done")
        mv_done = sem("mv_done")
        var_ready = sem("var_ready")
        rstd_ready = sem("rstd_ready")
        nbias_ready = sem("nbias_ready")
        h_ready = sem("h_ready")
        hT_psum_s = sem("hT_psum_s")
        hT_psum_d = sem("hT_psum_d")
        hTs_ready = sem("hTs_ready")
        hTd_ready = sem("hTd_ready")
        q_psum = sem("q_psum")
        k_psum = sem("k_psum")
        v_psum = sem("v_psum")
        q_ready = sem("q_ready")
        k_ready = sem("k_ready")
        v_ready = sem("v_ready")
        s_psum = sem("s_psum")
        soft = sem("soft")
        ex_ready = sem("ex_ready")
        vT_ready = sem("vT_ready")
        aT_ready = sem("aT_ready")
        m_psum = sem("m_psum")
        m_ready = sem("m_ready")
        m_moved = sem("m_moved")
        edge_ready = sem("edge_ready")
        rows_psum = sem("rows_psum")
        same_ready = sem("same_ready")
        hot_ready = sem("hot_ready")
        earlier_ready = sem("earlier_ready")
        count_ready = sem("count_ready")
        moved_ready = sem("moved_ready")
        key_kept = sem("key_kept")
        sidx_ready = sem("sidx_ready")
        o_psum = sem("o_psum")
        o_ready = sem("o_ready")
        sum_psum = sem("sum_psum")
        sum_ready = sem("sum_ready")
        added = sem("added")

        node_in = [sem(f"node_in{u}") for u in range(2)]
        nstats = sem("nstats")
        nmv = sem("nmv")
        nvar = sem("nvar")
        nrstd = sem("nrstd")
        nbias_n = sem("nbias_n")
        nh = sem("nh")
        nh_out = [sem(f"nh_out{u}") for u in range(2)]
        nT_psum = sem("nT_psum")
        nT_ready = sem("nT_ready")
        nself_psum = sem("nself_psum")
        nself = sem("nself")
        nself_out = [sem(f"nself_out{u}") for u in range(2)]

        g2idx = sem("g2idx")
        gathered2 = [sem(f"gathered2_{u}") for u in range(2)]
        edge2 = sem("edge2")
        hot2 = sem("hot2")
        rT_psum = sem("rT_psum")
        rT_ready = sem("rT_ready")
        rows2_psum = sem("rows2_psum")
        y_psum = sem("y_psum")
        y_hot = sem("y_hot")
        y_sel = sem("y_sel")
        same2 = sem("same2")
        earlier2 = sem("earlier2")
        count2 = sem("count2")
        moved2 = sem("moved2")
        sidx2 = sem("sidx2")
        sum2_psum = sem("sum2_psum")
        sum2 = sem("sum2")
        added2 = sem("added2")

        fin_in = [sem(f"fin_in{u}") for u in range(2)]
        fin_done = sem("fin_done")
        fin_out = [sem(f"fin_out{u}") for u in range(2)]

        nx = [xg[:, 0:J, :], xg[:, J:2 * J, :]]
        nhb = [hg[:, 0:J, :], hg[:, J:2 * J, :]]
        nT = [hTs, hTd]
        nout = [out_e, summed]
        nst = [stats[:, 0:J, :], stats[:, J:2 * J, :]]
        nmvb = [mv[:, 0:J, :], mv[:, J:2 * J, :]]
        LOADS = 24

        @block.sync
        def _(sp):
            sp.dma_start(x1[0:N, :].rearrange("(a b) d -> a (b d)", a=80),
                         x.rearrange("(a b) d -> a (b d)", a=80)).then_inc(x1_set, 16)
            sp.wait_ge(pads_ready, 1)
            whole = E // COLS
            for i, t in enumerate((src, dst, et3, et8)):
                full = t[0:whole * COLS].rearrange("(p c) -> p c", c=COLS)
                sp.dma_start(raw[0:112, i, :], full[0:112, :]).then_inc(loaded, 16)
                sp.dma_start(raw[112:whole, i, :], full[112:whole, :]).then_inc(loaded, 16)
                sp.dma_start(raw[whole:whole + 1, i, 0:E - whole * COLS],
                             t[whole * COLS:E].rearrange("(a c) -> a c", a=1)).then_inc(loaded, 16)
            sp.dma_start(x1[N:N + P, :], zeros[:]).then_inc(x1_set, 16)
            sp.dma_start(x1[N + P:ROWS, :], zeros[0:ROWS - N - P, :]).then_inc(x1_set, 16)

            def move_messages(b):
                if is_past(b, 1):
                    sp.wait_ge(o_psum, b)
                sp.wait_ge(m_ready, b + 1)
                for j in range(J):
                    for q in range(4):
                        sp.dma_start(m_dense[DH * q:DH * (q + 1), :, j, :],
                                     m_strip[DH * j:DH * (j + 1), q::4, :]).then_inc(m_moved, 16)

            move_messages(0)
            with sp.Fori(2, NB) as i:
                move_messages(i - 1)
            move_messages(NB - 1)

            def node_rows(t, n):
                return t[bass.ds(n * (P * J), P * J), :].rearrange("(p k) d -> p k d", k=J)

            def node_load(n, u, first):
                if not first:
                    sp.wait_ge(nh, J * (n - 1))
                sp.dma_start(nx[u], node_rows(x1, n)).then_inc(node_in[u], 16)

            def node_store(n, u):
                sp.wait_ge(nh, J * (n + 1))
                sp.dma_start(node_rows(h2, n), nhb[u]).then_inc(nh_out[u], 16)
                sp.wait_ge(nself, n + 1)
                sp.dma_start(node_rows(agg, n), nout[u][:]).then_inc(nself_out[u], 16)

            sp.wait_ge(added, 16 * J * NB)
            node_load(0, 0, True)
            node_load(1, 1, True)
            with sp.Fori(0, NB - 3, 2) as n:
                for u in range(2):
                    node_load(n + 2 + u, u, False)
                    node_store(n + u, u)
            for u in range(2):
                node_store(NB - 2 + u, u)

            def fin_load(n, u, parts, first):
                if not first:
                    sp.wait_ge(fin_done, n - 1)
                sp.dma_start(nx[u][0:parts], node_part(x1, n, parts)).then_inc(fin_in[u], 16)
                sp.dma_start(nhb[u][0:parts], node_part(agg, n, parts)).then_inc(fin_in[u], 16)

            def node_part(t, n, parts):
                return t[bass.ds(n * (P * J), parts * J), :].rearrange("(p k) d -> p k d", k=J)

            def fin_store(n, u, parts):
                sp.wait_ge(fin_done, n + 1)
                sp.dma_start(node_part(out, n, parts), nout[u][0:parts]).then_inc(fin_out[u], 16)

            last_parts = (N - (NB - 1) * P * J) // J
            sp.wait_ge(added2, 16 * J * NB)
            fin_load(0, 0, P, True)
            fin_load(1, 1, P, True)
            with sp.Fori(0, NB - 5, 2) as n:
                for u in range(2):
                    fin_load(n + 2 + u, u, P, False)
                    fin_store(n + u, u, P)
            fin_load(NB - 2, 0, P, False)
            fin_store(NB - 4, 0, P)
            fin_load(NB - 1, 1, last_parts, False)
            fin_store(NB - 3, 1, P)
            fin_store(NB - 2, 0, P)
            fin_store(NB - 1, 1, last_parts)
            for u in range(2):
                sp.wait_ge(fin_out[u], 16 * (NB // 2))

        @block.gpsimd
        def _(pool):
            nc.gpsimd.iota(dump[:], [[0, COLS]], base=N, channel_multiplier=1).then_inc(const_pool, 1)
            nc.gpsimd.iota(col_less_row[:], [[1, P]], base=0, channel_multiplier=-1).then_inc(const_pool, 1)
            nc.gpsimd.iota(edge_of_row[:], [[0, EG]], base=0, channel_multiplier=1).then_inc(const_pool, 1)
            nc.gpsimd.iota(edge_no[:], [[1, EG]], base=0, channel_multiplier=0).then_inc(const_pool, 1)
            nc.gpsimd.iota(rel_no[:], [[1, R]], base=0, channel_multiplier=0).then_inc(const_pool, 1)
            nc.gpsimd.iota(part_no[:], [[0, 1]], base=0, channel_multiplier=1).then_inc(const_pool, 1)
            nc.gpsimd.memset(minus_half[:], -0.5).then_inc(const_pool, 1)
            pool.wait_ge(const_pool, 7)

            def norm_scale(b):
                pool.wait_ge(var_ready, b + 1)
                if is_past(b, 1):
                    pool.wait_ge(h_ready, 2 * J * b)
                nc.gpsimd.tensor_tensor(rstd[:], var_e[:], minus_half[:], ALU.pow).then_inc(rstd_ready, 1)

            def gather(b, slots):
                for s in slots:
                    nc.gpsimd.indirect_dma_start(
                        xg[:, s, :], None, x,
                        bass.IndirectOffsetOnAxis(ap=g_idx[:, s:s + 1], axis=0)).then_inc(gathered, 16)

            def gather_may_start(b):
                now, before = counts(pool, b + 1, 2 * J * b)
                pool.wait_ge(const_pool, 7)
                pool.wait_ge(gidx_ready, now)
                if is_past(b, 1):
                    pool.wait_ge(h_ready, before)

            def scatter(b, j):
                before, = counts(pool, 16 * (J * b + j))
                pool.wait_ge(const_pool, 7)
                if is_past(b, 1) or j > 0:
                    pool.wait_ge(added, before)
                nc.gpsimd.indirect_dma_start(
                    x1, bass.IndirectOffsetOnAxis(ap=s_idx[:, j:j + 1], axis=0),
                    summed[:, j, :], None, compute_op=ALU.add).then_inc(added, 16)

            def body(i, scat, gath, norm):
                if norm:
                    norm_scale(i + 1)
                if gath:
                    gather_may_start(i + 2)
                    gather(i + 2, range(0, 4))
                if scat:
                    pool.wait_ge(sum_ready, i - 1)
                    pool.wait_ge(sidx_ready, i - 1)
                for j in range(J):
                    if scat:
                        scatter(i - 2, j)
                    if gath:
                        gather(i + 2, [4 + j])

            gather_may_start(0)
            gather(0, range(2 * J))
            norm_scale(0)
            gather_may_start(1)
            gather(1, range(2 * J))
            body(0, False, True, True)
            body(1, False, True, True)
            pool.wait_ge(x1_set, 48)
            with pool.Fori(2, NB - 2) as i:
                body(i, True, True, True)
            body(NB - 2, True, False, True)
            body(NB - 1, True, False, False)
            body(NB, True, False, False)
            body(NB + 1, True, False, False)

            def node_scale(n, u):
                pool.wait_ge(nvar, n + 1)
                nc.gpsimd.tensor_tensor(rstd[:, J * u:J * (u + 1)], var_e[:, J * u:J * (u + 1)],
                                        minus_half[:, 0:J], ALU.pow).then_inc(nrstd, 1)

            with pool.Fori(0, NB - 1, 2) as n:
                for u in range(2):
                    node_scale(n + u, u)

            def gather2(b, u, j):
                nc.gpsimd.indirect_dma_start(
                    xg[:, J * u + j, :], None, h2,
                    bass.IndirectOffsetOnAxis(ap=g_idx[:, J * u + j:J * u + j + 1], axis=0)
                ).then_inc(gathered2[u], 16)

            def gather2_may_start(b, u):
                now, before = counts(pool, b + 1, b - 1)
                pool.wait_ge(const_pool, 7)
                pool.wait_ge(g2idx, now)
                if is_past(b, 2):
                    pool.wait_ge(rT_psum, before)

            def scatter2(b, j):
                before, = counts(pool, 16 * (J * b + j))
                pool.wait_ge(const_pool, 7)
                if is_past(b, 1) or j > 0:
                    pool.wait_ge(added2, before)
                nc.gpsimd.indirect_dma_start(
                    agg, bass.IndirectOffsetOnAxis(ap=s_idx[:, j:j + 1], axis=0),
                    summed[:, j, :], None, compute_op=ALU.add).then_inc(added2, 16)

            def body2(b, u, gath):
                if gath:
                    gather2_may_start(b + 2, u)
                pool.wait_ge(sum2, b + 1)
                pool.wait_ge(sidx2, b + 1)
                for j in range(J):
                    scatter2(b, j)
                    if gath:
                        gather2(b + 2, u, j)

            for u in range(2):
                pool.wait_ge(nh_out[u], 16 * (NB // 2))
                pool.wait_ge(nself_out[u], 16 * (NB // 2))
            for u in range(2):
                gather2_may_start(u, u)
                for j in range(J):
                    gather2(u, u, j)
            with pool.Fori(0, NB - 3, 2) as b:
                for u in range(2):
                    body2(b + u, u, True)
            for u in range(2):
                body2(NB - 2 + u, u, False)

        @block.vector
        def _(dve):
            prep_n = [0]

            def then(ins):
                prep_n[0] += 1
                ins.then_inc(prep, 1)
                dve.wait_ge(prep, prep_n[0])

            nc.vector.memset(zeros[:], 0.0)
            dve.wait_ge(const_pool, 7)
            for i in range(2):
                nc.vector.tensor_copy(raw[:, i, :], dump[:])
            then(nc.vector.memset(raw[:, 2:4, :], 0))
            nc.vector.tensor_scalar(ident[:], col_less_row[:], 0.0, None, ALU.is_equal).then_inc(pads_ready, 1)
            nc.vector.tensor_scalar(lower[:], col_less_row[:], 0.0, None, ALU.is_lt)
            nc.vector.tensor_copy(part_f[:], part_no[:])
            then(nc.vector.tensor_scalar(edge_of_row[:], edge_of_row[:], EG - 1, None, ALU.bitwise_and))
            nc.vector.tensor_tensor(own_edge[:], edge_of_row[:], edge_no[:], ALU.is_equal).then_inc(const_ready, 1)

            dve.wait_ge(loaded, 16 * LOADS)

            def by_batch(t):
                return t.rearrange("p (b j) -> p b j", j=J)
            for s in range(2):
                key = by_batch(raw[:, s, :])
                tab = (src_tab, dst_tab)[s]
                nc.vector.scalar_tensor_tensor(gather_idx[:, :, J * s:J * (s + 1)], key, float(N), key,
                                               ALU.is_lt, ALU.mult)
                nc.vector.tensor_copy(tab[:, :, 0:J], key)
                nc.vector.tensor_tensor(tab[:, :, J:2 * J], by_batch(dump[:]), key, ALU.subtract)
                then(nc.vector.tensor_copy(tab[:, :, 2 * J:3 * J], by_batch(raw[:, 2 + s, :])))
            dve.wait_ge(type_psum, 1)
            nc.vector.tensor_tensor(type_out[:], ps_d[0:T3, 0:D], bo3[:], ALU.add).then_inc(type_ready, 1)

            def heads_first(t):
                return t[:].rearrange("p (g h e) -> p h g e", h=H, e=EG)

            def in_psum(t):
                return t[:].rearrange("p (h g e) -> p h g e", h=H, e=EG)

            def gather_rows(b):
                nc.vector.tensor_copy(g_idx[:], gather_idx[:, bass.ds(b, 1), :].rearrange("p b j -> p (b j)")
                                      ).then_inc(gidx_ready, 1)

            def moments(b):
                dve.wait_ge(gathered, 16 * 2 * J * (b + 1))
                for s in range(2 * J):
                    nc.vector.bn_stats(stats[:, s, :], xg[:, s, :]).then_inc(stats_done, 1)
                here, before = counts(dve, 2 * J * (b + 1), b)
                dve.wait_ge(const_pool, 7)
                dve.wait_ge(stats_done, here)
                if is_past(b, 1):
                    dve.wait_ge(nbias_ready, before)
                for s in range(2 * J):
                    nc.vector.bn_aggr(mv[:, s, :], stats[:, s, :]).then_inc(mv_done, 1)
                dve.wait_ge(mv_done, 2 * J * (b + 1))
                nc.vector.tensor_scalar(var_e[:], mv[:, :, 1], EPS, None, ALU.add).then_inc(var_ready, 1)

            def norm_bias(b):
                dve.wait_ge(rstd_ready, b + 1)
                nc.vector.scalar_tensor_tensor(nbias[:], mv[:, :, 0], -1.0, rstd[:], ALU.mult, ALU.mult
                                               ).then_inc(nbias_ready, 1)

            def softmax(b):
                sv = ps_a[:].rearrange("p (n e) -> p n e", e=EG)
                ov = own_sc[:].rearrange("p (n e) -> p n e", e=EG)
                av = a_tok[:].rearrange("p (n e) -> p n e", e=EG)
                own = own_edge[:].unsqueeze(1).to_broadcast([P, G * H, EG])
                dve.wait_ge(s_psum, b + 1)
                nc.vector.tensor_tensor(ov, sv, own, ALU.mult).then_inc(soft, 1)
                dve.wait_ge(soft, 8 * b + 1)
                nc.vector.tensor_reduce(sc[:].rearrange("p g h -> p (g h)"), ov, AX.X, ALU.add).then_inc(soft, 1)
                dve.wait_ge(soft, 8 * b + 2)
                nc.vector.tensor_reduce(mx[:], sc[:], AX.X, ALU.max).then_inc(soft, 1)
                dve.wait_ge(soft, 8 * b + 3)
                nc.vector.tensor_tensor(cen[:], sc[:], mx[:].unsqueeze(2).to_broadcast([P, G, H]), ALU.subtract
                                        ).then_inc(soft, 1)
                dve.wait_ge(ex_ready, b + 1)
                nc.vector.tensor_reduce(den[:], ex[:], AX.X, ALU.add).then_inc(soft, 1)
                dve.wait_ge(soft, 8 * b + 5)
                nc.vector.reciprocal(rden[:], den[:]).then_inc(soft, 1)
                dve.wait_ge(soft, 8 * b + 6)
                nc.vector.tensor_tensor(pr[:], ex[:], rden[:].unsqueeze(2).to_broadcast([P, G, H]), ALU.mult
                                        ).then_inc(soft, 1)
                dve.wait_ge(soft, 8 * b + 7)
                nc.vector.tensor_tensor(av, pr[:].rearrange("p g h -> p (g h)").unsqueeze(2).to_broadcast([P, G * H, EG]),
                                        own, ALU.mult).then_inc(soft, 1)

            def turn(b):
                if is_past(b, 1):
                    dve.wait_ge(m_psum, b)
                dve.wait_ge(v_ready, H * (b + 1))
                nc.vector.transpose(vT[:], v_tok[:]).then_inc(vT_ready, 1)
                dve.wait_ge(soft, 8 * (b + 1))
                nc.vector.transpose(aT[:], a_tok[:]).then_inc(aT_ready, 1)

            def project(b):
                dve.wait_ge(q_psum, b + 1)
                nc.vector.tensor_tensor(heads_first(q_tok), in_psum(ps_c),
                                        bq[:].unsqueeze(2).unsqueeze(3).to_broadcast([P, H, G, EG]), ALU.add
                                        ).then_inc(q_ready, 1)
                dve.wait_ge(k_psum, b + 1)
                nc.vector.tensor_tensor(heads_first(k_tok), in_psum(ps_b),
                                        bk[:].unsqueeze(2).unsqueeze(3).to_broadcast([P, H, G, EG]), ALU.add
                                        ).then_inc(k_ready, 1)

            def stage_edges(b):
                if is_past(b, 1):
                    dve.wait_ge(rows_psum, b)
                nc.vector.tensor_copy(edge_f[:], src_tab[:, bass.ds(b, 1), :].rearrange("p b j -> p (b j)")
                                      ).then_inc(edge_ready, 1)

            def repeats(b):
                dve.wait_ge(rows_psum, b + 1)
                if is_past(b, 1):
                    dve.wait_ge(sum_psum, b)
                nc.vector.tensor_tensor(same[:], ps_a[:, 0:512].rearrange("p (j e) -> p j e", j=J),
                                        edge_f[:, 0:J].unsqueeze(2).to_broadcast([P, J, P]), ALU.is_equal
                                        ).then_inc(same_ready, 1)
                if is_past(b, 1):
                    dve.wait_ge(o_psum, b)
                nc.vector.tensor_scalar(type_hot[:], ps_a[0:T3, 512:1024], part_f[0:T3, :], None, ALU.is_equal
                                        ).then_inc(hot_ready, 1)
                dve.wait_ge(same_ready, b + 1)
                nc.vector.tensor_tensor(earlier[:], same[:], lower[:].unsqueeze(1).to_broadcast([P, J, P]), ALU.mult
                                        ).then_inc(earlier_ready, 1)
                dve.wait_ge(earlier_ready, b + 1)
                nc.vector.tensor_reduce(count[:], earlier[:], AX.X, ALU.add).then_inc(count_ready, 1)
                dve.wait_ge(count_ready, b + 1)
                nc.vector.scalar_tensor_tensor(moved[:], count[:], 0.0, edge_f[:, J:2 * J], ALU.is_gt, ALU.mult
                                               ).then_inc(moved_ready, 1)
                dve.wait_ge(moved_ready, b + 1)
                nc.vector.tensor_tensor(s_key[:, 0:J], moved[:], edge_f[:, 0:J], ALU.add).then_inc(key_kept, 1)

            def scatter_rows(b):
                dve.wait_ge(key_kept, b + 1)
                if is_past(b, 1):
                    dve.wait_ge(added, 16 * J * b)
                nc.vector.tensor_copy(s_idx[:], s_key[:, 0:J]).then_inc(sidx_ready, 1)

            def body(i, nxt, nxt2, cur, prev, prev2):
                if nxt:
                    moments(i + 1)
                    if nxt2:
                        gather_rows(i + 2)
                if prev2:
                    scatter_rows(i - 2)
                if prev:
                    stage_edges(i - 1)
                if nxt:
                    norm_bias(i + 1)
                if cur:
                    softmax(i)
                    turn(i)
                if prev:
                    repeats(i - 1)
                if nxt:
                    project(i + 1)

            gather_rows(0)
            moments(0)
            gather_rows(1)
            norm_bias(0)
            project(0)
            body(0, True, True, True, False, False)
            body(1, True, True, True, True, False)
            with dve.Fori(2, NB - 2) as i:
                body(i, True, True, True, True, True)
            body(NB - 2, True, False, True, True, True)
            body(NB - 1, False, False, True, True, True)
            body(NB, False, False, False, True, True)
            body(NB + 1, False, False, False, False, True)

            def node_moments(n, u):
                dve.wait_ge(node_in[u], 16 * (n // 2 + 1) if isinstance(n, int) else n * 8 + 16 - 8 * u)
                for s in range(J):
                    nc.vector.bn_stats(nst[u][:, s, :], nx[u][:, s, :]).then_inc(nstats, 1)
                here, = counts(dve, J * (n + 1))
                dve.wait_ge(const_pool, 7)
                dve.wait_ge(nstats, here)
                for s in range(J):
                    nc.vector.bn_aggr(nmvb[u][:, s, :], nst[u][:, s, :]).then_inc(nmv, 1)
                dve.wait_ge(nmv, J * (n + 1))
                nc.vector.tensor_scalar(var_e[:, J * u:J * (u + 1)], nmvb[u][:, :, 1], EPS, None, ALU.add
                                        ).then_inc(nvar, 1)

            def node_bias(n, u):
                dve.wait_ge(nrstd, n + 1)
                if is_past(n, 2):
                    dve.wait_ge(nh, J * (n - 1))
                nc.vector.scalar_tensor_tensor(nbias[:, J * u:J * (u + 1)], nmvb[u][:, :, 0], -1.0,
                                               rstd[:, J * u:J * (u + 1)], ALU.mult, ALU.mult
                                               ).then_inc(nbias_n, 1)

            def node_self(n, u):
                dve.wait_ge(nself_psum, n + 1)
                if is_past(n, 2):
                    dve.wait_ge(nself_out[u], n * 8 - 8 * u)
                nc.vector.tensor_tensor(nout[u][:], ps_c[:, 512 * u:512 * (u + 1)].rearrange("p (k d) -> p k d", k=J),
                                        b_self[:].unsqueeze(1).to_broadcast([P, J, D]), ALU.add
                                        ).then_inc(nself, 1)

            def node_body(n, u, nxt):
                if nxt:
                    node_moments(n + 1, 1 - u)
                    node_bias(n + 1, 1 - u)
                node_self(n, u)

            node_moments(0, 0)
            node_bias(0, 0)
            node_body(0, 0, True)
            node_body(1, 1, True)
            with dve.Fori(2, NB - 3, 2) as n:
                for u in range(2):
                    node_body(n + u, u, True)
            node_body(NB - 2, 0, True)
            node_body(NB - 1, 1, False)

            def gather2_rows(b, u):
                if is_past(b, 2):
                    dve.wait_ge(gathered2[u], 16 * J * (b // 2) if isinstance(b, int) else b * 32 - 32 * u)
                nc.vector.tensor_copy(g_idx[:, J * u:J * (u + 1)],
                                      gather_idx[:, bass.ds(b, 1), 0:J].rearrange("p b j -> p (b j)")
                                      ).then_inc(g2idx, 1)

            def relation(b, u):
                if is_past(b, 1):
                    dve.wait_ge(rows2_psum, b)
                    dve.wait_ge(sidx2, b)
                nc.vector.tensor_copy(edge_f[:], dst_tab[:, bass.ds(b, 1), :].rearrange("p b j -> p (b j)")
                                      ).then_inc(edge2, 1)
                dve.wait_ge(edge2, b + 1)
                nc.vector.tensor_tensor(hot[:], edge_f[:, 2 * J:3 * J].unsqueeze(2).to_broadcast([P, J, R]),
                                        rel_no[:].unsqueeze(1).to_broadcast([P, J, R]), ALU.is_equal
                                        ).then_inc(hot2, 1)
                dve.wait_ge(rows2_psum, b + 1)
                if is_past(b, 1):
                    dve.wait_ge(sum2_psum, b)
                nc.vector.tensor_tensor(same[:], ps_e[:].rearrange("p (j e) -> p j e", j=J),
                                        edge_f[:, 0:J].unsqueeze(2).to_broadcast([P, J, P]), ALU.is_equal
                                        ).then_inc(same2, 1)
                dve.wait_ge(same2, b + 1)
                nc.vector.tensor_tensor(earlier[:], same[:], lower[:].unsqueeze(1).to_broadcast([P, J, P]), ALU.mult
                                        ).then_inc(earlier2, 1)
                dve.wait_ge(earlier2, b + 1)
                nc.vector.tensor_reduce(count[:], earlier[:], AX.X, ALU.add).then_inc(count2, 1)
                dve.wait_ge(count2, b + 1)
                nc.vector.scalar_tensor_tensor(moved[:], count[:], 0.0, edge_f[:, J:2 * J], ALU.is_gt, ALU.mult
                                               ).then_inc(moved2, 1)
                dve.wait_ge(hot2, b + 1)
                for j in range(J):
                    dve.wait_ge(y_psum, J * b + j + 1)
                    y = (ps_a, ps_b)[j % 2]
                    nc.vector.tensor_tensor(picked[j % 2][:].rearrange("p (o r) -> p r o", r=R),
                                            y[:].rearrange("p (r o) -> p r o", r=R),
                                            hot[:, j, :].unsqueeze(2).to_broadcast([P, R, D]), ALU.mult
                                            ).then_inc(y_hot, 1)
                    dve.wait_ge(y_hot, J * b + j + 1)
                    nc.vector.tensor_reduce(out_e[:, j, :], picked[j % 2][:].rearrange("p (o r) -> p o r", r=R),
                                            AX.X, ALU.add).then_inc(y_sel, 1)
                dve.wait_ge(moved2, b + 1)
                if is_past(b, 1):
                    dve.wait_ge(added2, 16 * J * b)
                nc.vector.tensor_tensor(s_idx[:], moved[:], edge_f[:, 0:J], ALU.add).then_inc(sidx2, 1)

            hot = cen[:, 0:J, :]
            picked = [q_tok, k_tok]
            gather2_rows(0, 0)
            gather2_rows(1, 1)
            for u in range(2):
                relation(u, u)
                gather2_rows(2 + u, u)
            with dve.Fori(2, NB - 3, 2) as b:
                for u in range(2):
                    relation(b + u, u)
                    gather2_rows(b + u + 2, u)
            for u in range(2):
                relation(NB - 2 + u, u)

            def fin(n, u, parts):
                dve.wait_ge(fin_in[u], n * 16 + 32 - 16 * u)
                if is_past(n, 2):
                    dve.wait_ge(fin_out[u], n * 8 - 8 * u)
                nc.vector.scalar_tensor_tensor(nout[u][0:parts], nhb[u][0:parts], 0.0, nx[u][0:parts],
                                               ALU.max, ALU.add).then_inc(fin_done, 1)

            fin(0, 0, P)
            fin(1, 1, P)
            with dve.Fori(2, NB - 3, 2) as n:
                for u in range(2):
                    fin(n + u, u, P)
            fin(NB - 2, 0, P)
            fin(NB - 1, 1, (N - (NB - 1) * P * J) // J)

        @block.scalar
        def _(act):
            act.dma_start(wq[:], wqT).then_inc(loaded, 16)
            act.dma_start(wk[:], wkT).then_inc(loaded, 16)
            act.dma_start(wv[:], wvT).then_inc(loaded, 16)
            act.dma_start(wo[:], woT.rearrange("(a p) o -> p a o", p=P)).then_inc(loaded, 16)
            act.dma_start(emb[:], embT.rearrange("(a p) t -> p a t", p=P)).then_inc(loaded, 16)
            act.dma_start(bo3[:], bo.rearrange("(a d) -> a d", a=1).to_broadcast([T3, D])).then_inc(loaded, 16)
            act.dma_start(w_rel[:], wrel.rearrange("r d o -> d r o")).then_inc(loaded, 16)
            act.dma_start(w_self[:], wself).then_inc(loaded, 16)
            act.dma_start(b_self[:], bias1.rearrange("(a d) -> a d", a=1).to_broadcast([P, D])).then_inc(loaded, 16)
            for t, b in ((bq, bqT), (bk, bkT), (bv, bvT)):
                act.dma_start(t[:], b).then_inc(loaded, 16)

            def normalise(b):
                act.wait_ge(nbias_ready, b + 1)
                if is_past(b, 1):
                    act.wait_ge(hT_psum_d, b)
                for s in range(2 * J):
                    nc.scalar.activation(hg[:, s, :], xg[:, s, :], ACT.Relu, scale=rstd[:, s:s + 1],
                                         bias=nbias[:, s:s + 1]).then_inc(h_ready, 1)

            def tile_sums(b):
                act.wait_ge(sum_psum, b + 1)
                if is_past(b, 1):
                    act.wait_ge(added, 16 * J * b)
                nc.scalar.copy(summed[:].rearrange("p j d -> p (j d)"), ps_e[:]).then_inc(sum_ready, 1)

            def exponent(b):
                act.wait_ge(soft, 8 * b + 4)
                nc.scalar.activation(ex[:], cen[:], ACT.Exp, scale=SCALE).then_inc(ex_ready, 1)

            def messages(b):
                act.wait_ge(m_psum, b + 1)
                if is_past(b, 1):
                    act.wait_ge(m_moved, 256 * b)
                nc.scalar.copy(m_strip[:].rearrange("p h (g e) -> p h g e", e=EG),
                               ps_b[:].rearrange("p (g h e) -> p h g e", h=H, e=EG)).then_inc(m_ready, 1)

            def turned(b):
                act.wait_ge(hT_psum_s, b + 1)
                nc.scalar.copy(hTs[:], ps_d[:]).then_inc(hTs_ready, 1)
                act.wait_ge(hT_psum_d, b + 1)
                nc.scalar.copy(hTd[:], ps_e[:]).then_inc(hTd_ready, 1)

            def values(b):
                act.wait_ge(v_psum, b + 1)
                if is_past(b, 1):
                    act.wait_ge(vT_ready, b)
                vv = v_tok[:].rearrange("p (g h e) -> p h g e", h=H, e=EG)
                for h in range(H):
                    nc.scalar.activation(vv[:, h], ps_c[:, P * h:P * (h + 1)].rearrange("p (g e) -> p g e", e=EG),
                                         ACT.Identity, bias=bv[:, h:h + 1]).then_inc(v_ready, 1)

            def edge_out(b):
                act.wait_ge(o_psum, b + 1)
                if is_past(b, 1):
                    act.wait_ge(sum_psum, b)
                nc.scalar.copy(out_e[:].rearrange("p j d -> p (j d)"), ps_d[:]).then_inc(o_ready, 1)

            def body(i, nxt, cur, prev, prev2):
                if nxt:
                    normalise(i + 1)
                if prev2:
                    tile_sums(i - 2)
                if cur:
                    exponent(i)
                if prev:
                    messages(i - 1)
                if nxt:
                    turned(i + 1)
                    values(i + 1)
                if prev:
                    edge_out(i - 1)

            act.wait_ge(loaded, 16 * LOADS)
            normalise(0)
            turned(0)
            values(0)
            body(0, True, True, False, False)
            body(1, True, True, True, False)
            with act.Fori(2, NB - 1) as i:
                body(i, True, True, True, True)
            body(NB - 1, False, True, True, True)
            body(NB, False, False, True, True)
            body(NB + 1, False, False, False, True)

            def node(n, u):
                act.wait_ge(nbias_n, n + 1)
                if is_past(n, 2):
                    act.wait_ge(nh_out[u], n * 8 - 8 * u)
                    act.wait_ge(nT_psum, n - 1)
                for s in range(J):
                    nc.scalar.activation(nhb[u][:, s, :], nx[u][:, s, :], ACT.Relu,
                                         scale=rstd[:, J * u + s:J * u + s + 1],
                                         bias=nbias[:, J * u + s:J * u + s + 1]).then_inc(nh, 1)
                act.wait_ge(nT_psum, n + 1)
                if is_past(n, 2):
                    act.wait_ge(nself_psum, n - 1)
                nc.scalar.copy(nT[u][:], (ps_d, ps_e)[u][:]).then_inc(nT_ready, 1)

            node(0, 0)
            node(1, 1)
            with act.Fori(2, NB - 1, 2) as n:
                for u in range(2):
                    node(n + u, u)

            def relation(b, u):
                act.wait_ge(rT_psum, b + 1)
                if is_past(b, 1):
                    act.wait_ge(y_psum, J * b)
                nc.scalar.copy(hTs[:], ps_d[:]).then_inc(rT_ready, 1)
                act.wait_ge(sum2_psum, b + 1)
                if is_past(b, 1):
                    act.wait_ge(added2, 16 * J * b)
                nc.scalar.copy(summed[:].rearrange("p j d -> p (j d)"), ps_c[:, 0:512]).then_inc(sum2, 1)

            relation(0, 0)
            relation(1, 1)
            with act.Fori(2, NB - 1, 2) as b:
                for u in range(2):
                    relation(b + u, u)

        @block.tensor
        def _(pe):
            pe.wait_ge(loaded, 16 * LOADS)
            pe.wait_ge(const_ready, 1)
            for a in range(2):
                last = nc.tensor.matmul(ps_d[0:T3, 0:D], emb[:, a, :], wo[:, a, :], start=(a == 0), stop=(a == 1))
            last.then_inc(type_psum, 1)
            pe.wait_ge(type_ready, 1)

            def turn(b):
                pe.wait_ge(h_ready, 2 * J * (b + 1))
                if is_past(b, 3):
                    pe.wait_ge(o_ready, b - 2)
                for j in range(J):
                    last = nc.tensor.transpose(ps_d[:, P * j:P * (j + 1)], hg[:, j, :], ident[:])
                last.then_inc(hT_psum_s, 1)
                if is_past(b, 3):
                    pe.wait_ge(sum_ready, b - 2)
                for j in range(J):
                    last = nc.tensor.transpose(ps_e[:, P * j:P * (j + 1)], hg[:, J + j, :], ident[:])
                last.then_inc(hT_psum_d, 1)

            def projection(dest, w, hT, done):
                for h in range(H):
                    for j in range(J):
                        last = nc.tensor.matmul(dest[DH * j:DH * (j + 1), P * h:P * (h + 1)],
                                                w[:, DH * h:DH * (h + 1)], hT[:, P * j:P * (j + 1)],
                                                start=True, stop=True)
                last.then_inc(done, 1)

            def project(b):
                pe.wait_ge(hTs_ready, b + 1)
                if is_past(b, 1):
                    pe.wait_ge(v_ready, H * b)
                projection(ps_c, wq, hTs, q_psum)
                pe.wait_ge(hTd_ready, b + 1)
                if is_past(b, 2):
                    pe.wait_ge(m_ready, b - 1)
                projection(ps_b, wk, hTd, k_psum)
                pe.wait_ge(q_ready, b + 1)
                projection(ps_c, wv, hTd, v_psum)

            def scores(b):
                now, before = counts(pe, b + 1, b - 1)
                pe.wait_ge(const_ready, 1)
                pe.wait_ge(k_ready, now)
                if is_past(b, 2):
                    pe.wait_ge(hot_ready, before)
                for g in range(G):
                    for j in range(J):
                        s, t = slice(DH * j, DH * (j + 1)), slice(TOK * g, TOK * (g + 1))
                        last = nc.tensor.matmul(ps_a[s, t], q_tok[s, t], k_tok[s, t], start=True, stop=True)
                last.then_inc(s_psum, 1)

            def messages(b):
                now, = counts(pe, b + 1)
                pe.wait_ge(const_ready, 1)
                pe.wait_ge(aT_ready, now)
                pe.wait_ge(vT_ready, now)
                for g in range(G):
                    for j in range(J):
                        s, t = slice(DH * j, DH * (j + 1)), slice(TOK * g, TOK * (g + 1))
                        last = nc.tensor.matmul(ps_b[s, t], vT[s, t], aT[s, t], start=True, stop=True)
                last.then_inc(m_psum, 1)

            def rows(b):
                pe.wait_ge(edge_ready, b + 1)
                pe.wait_ge(soft, 8 * (b + 1) + 1)
                for f in (0, 1):
                    for j in range(J):
                        c = 2 * J * f + j
                        last = nc.tensor.transpose(ps_a[:, 512 * f + P * j:512 * f + P * (j + 1)],
                                                   edge_f[:, c:c + 1].to_broadcast([P, P]), ident[:])
                last.then_inc(rows_psum, 1)

            def edge_out(b):
                pe.wait_ge(m_moved, 256 * (b + 1))
                pe.wait_ge(hot_ready, b + 1)
                for j in range(J):
                    o = ps_d[:, P * j:P * (j + 1)]
                    nc.tensor.matmul(o, m_dense[:, 0, j, :], wo[:, 0, :], start=True, stop=False)
                    nc.tensor.matmul(o, m_dense[:, 1, j, :], wo[:, 1, :], start=False, stop=False)
                    last = nc.tensor.matmul(o, type_hot[:, P * j:P * (j + 1)], type_out[:], start=False, stop=True)
                last.then_inc(o_psum, 1)

            def tile_sums(b):
                pe.wait_ge(o_ready, b + 1)
                pe.wait_ge(same_ready, b + 1)
                for j in range(J):
                    last = nc.tensor.matmul(ps_e[:, P * j:P * (j + 1)], same[:, j, :], out_e[:, j, :],
                                            start=True, stop=True)
                last.then_inc(sum_psum, 1)

            def body(i, nxt, cur, prev, prev2):
                if cur:
                    scores(i)
                if prev2:
                    tile_sums(i - 2)
                if prev:
                    messages(i - 1)
                    if cur:
                        rows(i - 1)
                    else:
                        rows_last(i - 1)
                if nxt:
                    turn(i + 1)
                    project(i + 1)
                if prev:
                    edge_out(i - 1)

            def rows_last(b):
                pe.wait_ge(edge_ready, b + 1)
                pe.wait_ge(hot_ready, b)
                for f in (0, 1):
                    for j in range(J):
                        c = 2 * J * f + j
                        last = nc.tensor.transpose(ps_a[:, 512 * f + P * j:512 * f + P * (j + 1)],
                                                   edge_f[:, c:c + 1].to_broadcast([P, P]), ident[:])
                last.then_inc(rows_psum, 1)

            turn(0)
            project(0)
            body(0, True, True, False, False)
            body(1, True, True, True, False)
            with pe.Fori(2, NB - 1) as i:
                body(i, True, True, True, True)
            body(NB - 1, False, True, True, True)
            body(NB, False, False, True, True)
            body(NB + 1, False, False, False, True)

            def node(n, u):
                pe.wait_ge(nh, J * (n + 1))
                if is_past(n, 2):
                    pe.wait_ge(nT_ready, n - 1)
                ps = (ps_d, ps_e)[u]
                for j in range(J):
                    last = nc.tensor.transpose(ps[:, P * j:P * (j + 1)], nhb[u][:, j, :], ident[:])
                last.then_inc(nT_psum, 1)
                pe.wait_ge(nT_ready, n + 1)
                if is_past(n, 2):
                    pe.wait_ge(nself, n - 1)
                for j in range(J):
                    last = nc.tensor.matmul(ps_c[:, 512 * u + P * j:512 * u + P * (j + 1)],
                                            nT[u][:, P * j:P * (j + 1)], w_self[:], start=True, stop=True)
                last.then_inc(nself_psum, 1)

            node(0, 0)
            node(1, 1)
            with pe.Fori(2, NB - 1, 2) as n:
                for u in range(2):
                    node(n + u, u)

            def rel_turn(b, u):
                pe.wait_ge(gathered2[u], 16 * J * (b // 2 + 1) if isinstance(b, int) else b * 32 + 64 - 32 * u)
                if is_past(b, 1):
                    pe.wait_ge(rT_ready, b)
                for j in range(J):
                    last = nc.tensor.transpose(ps_d[:, P * j:P * (j + 1)], xg[:, J * u + j, :], ident[:])
                last.then_inc(rT_psum, 1)

            def rel_rows(b):
                pe.wait_ge(edge2, b + 1)
                if is_past(b, 1):
                    pe.wait_ge(same2, b)
                for j in range(J):
                    last = nc.tensor.transpose(ps_e[:, P * j:P * (j + 1)],
                                               edge_f[:, j:j + 1].to_broadcast([P, P]), ident[:])
                last.then_inc(rows2_psum, 1)

            def rel_products(b):
                pe.wait_ge(rT_ready, b + 1)
                for j in range(J):
                    if is_past(b, 1) or j >= 2:
                        pe.wait_ge(y_hot, J * b + j - 1)
                    y = (ps_a, ps_b)[j % 2]
                    for a in range(2):
                        last = nc.tensor.matmul(y[:, 512 * a:512 * (a + 1)], hTs[:, P * j:P * (j + 1)],
                                                w_rel[:, 4 * a:4 * (a + 1), :].rearrange("p r o -> p (r o)"),
                                                start=True, stop=True)
                    last.then_inc(y_psum, 1)

            def rel_sums(b):
                pe.wait_ge(y_sel, J * (b + 1))
                pe.wait_ge(same2, b + 1)
                if is_past(b, 1):
                    pe.wait_ge(sum2, b)
                for j in range(J):
                    last = nc.tensor.matmul(ps_c[:, P * j:P * (j + 1)], same[:, j, :], out_e[:, j, :],
                                            start=True, stop=True)
                last.then_inc(sum2_psum, 1)

            def rel_body(b, u):
                rel_turn(b, u)
                rel_rows(b)
                rel_products(b)
                rel_sums(b)

            rel_body(0, 0)
            rel_body(1, 1)
            with pe.Fori(2, NB - 1, 2) as b:
                for u in range(2):
                    rel_body(b + u, u)


def kernel(**inputs):
    import numpy as np
    import concourse.bacc as bacc
    from concourse import mybir as mb
    from concourse.bass_utils import run_bass_kernel_spmd

    def turned(name):
        return np.ascontiguousarray(np.asarray(inputs[name]).T)

    def by_head(name):
        return np.ascontiguousarray(np.tile(np.asarray(inputs[name]).reshape(H, DH).T, (4, 1)))

    def plain(name):
        return np.ascontiguousarray(inputs[name])

    given = {
        "x": plain("x"), "src": plain("src"), "dst": plain("dst"),
        "et3": plain("edge_type_3"), "et8": plain("edge_type_8"),
        "wqT": turned("L0_gnn_Wq"), "bqT": by_head("L0_gnn_bq"),
        "wkT": turned("L0_gnn_Wk"), "bkT": by_head("L0_gnn_bk"),
        "wvT": turned("L0_gnn_Wv"), "bvT": by_head("L0_gnn_bv"),
        "embT": turned("L0_gnn_edge_emb"), "woT": turned("L0_gnn_Wo"), "bo": plain("L0_gnn_bo"),
        "wrel": plain("L1_gnn_weight"), "wself": plain("L1_gnn_self_loop_weight"), "bias1": plain("L1_gnn_bias"),
    }
    nc = bacc.Bacc("TRN2", target_bir_lowering=False, num_devices=1)
    aps = {k: nc.dram_tensor(f"in_{k}", a.shape, mb.dt.from_np(a.dtype), kind="ExternalInput").ap()
           for k, a in given.items()}
    out = nc.dram_tensor("out", (N, D), mb.dt.float32, kind="ExternalOutput").ap()
    build(nc, *aps.values(), out)
    r = run_bass_kernel_spmd(nc, [{f"in_{k}": a for k, a in given.items()}], core_ids=[0])
    return r.results[0]["out"]
```

```python
import concourse.bass as bass
from concourse import mybir
from contextlib import ExitStack

F32 = mybir.dt.float32
I32 = mybir.dt.int32
ALU = mybir.AluOpType
ACT = mybir.ActivationFunctionType
AX = mybir.AxisListType

P = 128
D = 128
H = 8
DH = 32
HID = H * DH
N = 50000
E = 50000
T3 = 3
R = 8
J = 4
BF16 = mybir.dt.bfloat16
NT = 7
NB = -(-E // (P * J))
COLS = NB * J
ROWS = NB * P * J
EG = 4
G = P // EG
TOK = EG * H
NN = ROWS // (P * NT)
SPLIT = 3
EPS = 1e-5
SCALE = float(DH) ** -0.5


def is_past(b, k):
    return not isinstance(b, int) or b >= k


def exists(b, n=NB):
    return not isinstance(b, int) or 0 <= b < n


def counts(eng, *values):
    return [v if isinstance(v, int) else eng.to_reg(v) for v in values]


def build(nc, x, src, dst, et3, et8, wqT, bqR, wkT, bkR, wvT, bvR, embT, woT, bo, wrel, wself, bias1, out):
    x1 = nc.dram_tensor("x1", (ROWS, D), F32, kind="Internal").ap()
    h1 = nc.dram_tensor("h1", (ROWS, D), F32, kind="Internal").ap()
    h2 = nc.dram_tensor("h2", (ROWS, D), F32, kind="Internal").ap()
    agg = nc.dram_tensor("agg", (ROWS, D), F32, kind="Internal").ap()

    ctx = ExitStack()
    with ctx:
        def sb(name, shape, dt=F32):
            return ctx.enter_context(nc.sbuf_tensor(name, shape, dt))

        def sem(name):
            return ctx.enter_context(nc.semaphore(name))

        ident = sb("ident", [P, P])
        lower = sb("lower", [P, P])
        col_less_row = sb("col_less_row", [P, P], I32)
        ident_b = sb("ident_b", [P, P], BF16)
        own_edge = sb("own_edge", [P, EG])
        edge_of_row = sb("edge_of_row", [P, EG], I32)
        edge_no = sb("edge_no", [P, EG], I32)
        rel_no = sb("rel_no", [P, R], I32)
        part_no = sb("part_no", [P, 1], I32)
        part_f = sb("part_f", [P, 1])
        minus_half = sb("minus_half", [P, 2 * NT])
        zeros = sb("zeros", [P, D])
        wq = sb("wq", [P, HID])
        wk = sb("wk", [P, HID])
        wv = sb("wv", [P, HID])
        wo = sb("wo", [P, 2, D])
        emb = sb("emb", [P, 2, SPLIT * T3])
        BR = SPLIT * 4
        b_in = sb("b_in", [BR, 3, 2 * P])
        b_rows = sb("b_rows", [BR, 3, 2 * P], BF16)
        head_cols = sb("head_cols", [BR, 4, P], BF16)
        head_no = sb("head_no", [P, 4, P], I32)
        TR = SPLIT * T3
        bo_rows = sb("bo_rows", [TR, D])
        type_f = sb("type_f", [TR, 1, D])
        type_out = sb("type_out", [TR, 1, D], BF16)
        split_part = sb("split_part", [BR, 3, 2 * P], BF16)
        split_rest = sb("split_rest", [BR, 3, 2 * P])
        split_mask = sb("split_mask", [BR, SPLIT + 1])
        type_of_row = sb("type_of_row", [TR, 1])
        w_rel = sb("w_rel", [P, R, D])
        w_self = sb("w_self", [P, D])
        b_self = sb("b_self", [P, D])

        raw = sb("raw", [P, 4, COLS], I32)
        gather_idx = sb("gather_idx", [P, NB, 2 * J], I32)
        dump = sb("dump", [P, COLS], I32)
        src_tab = sb("src_tab", [P, NB, 3 * J])
        dst_tab = sb("dst_tab", [P, NB, 3 * J])
        src_parts = sb("src_parts", [P, NB, 3 * J], BF16)
        dst_parts = sb("dst_parts", [P, NB, 3 * J], BF16)
        key_bits = sb("key_bits", [P, COLS], I32)

        g_idx = sb("g_idx", [P, 2 * J], I32)
        stats = sb("stats", [P, 2 * NT, 6])
        mv = sb("mv", [P, 2 * NT, 2])
        var_e = sb("var_e", [P, 2 * NT])
        rstd = sb("rstd", [P, 2 * NT])
        nbias = sb("nbias", [P, 2 * NT])
        hg = sb("hg", [P, 2 * J, D])
        hTs = sb("hTs", [P, J * P])
        hTd = sb("hTd", [P, J * P])
        q_tok = sb("q_tok", [P, G * TOK])
        k_blk = sb("k_blk", [P, G, J, TOK])
        v_tok = sb("v_tok", [P, G * TOK])
        own_sc = sb("own_sc", [P, G * TOK])
        sc = sb("sc", [P, G, H])
        mx = sb("mx", [P, G])
        cen = sb("cen", [P, G, H])
        ex = sb("ex", [P, G, H])
        den = sb("den", [P, G])
        rden = sb("rden", [P, G])
        pr = sb("pr", [P, G, H])
        a_tok = sb("a_tok", [P, G * TOK])
        a_turned = sb("a_turned", [P, G, TOK])
        a_blk = sb("a_blk", [P, G, 4, TOK])
        vT = sb("vT", [P, G * TOK])
        m_strip = sb("m_strip", [P, H, P])
        m_dense = sb("m_dense", [P, 2, J, P])
        summed_b = sb("summed_b", [P, J, D])
        edge_f = sb("edge_f", [P, 3 * J])
        edge_f2 = sb("edge_f2", [P, 3 * J])
        edge_p = sb("edge_p", [P, 3 * J], BF16)
        edge_p2 = sb("edge_p2", [P, 3 * J], BF16)
        same = sb("same", [P, J, P])
        same_b = sb("same_b", [P, J, P])
        earlier = sb("earlier", [P, J, P])
        count = sb("count", [P, J])
        moved = sb("moved", [P, J])
        s_keys = sb("s_keys", [P, NB, J])
        s_idx = sb("s_idx", [P, J], I32)
        s_idx_b = sb("s_idx_b", [P, J], I32)
        type_hot = sb("type_hot", [TR, J * P], BF16)
        out_e = sb("out_e", [P, J, D])
        summed = sb("summed", [P, J, D])
        out_b = sb("out_b", [P, J, D])

        def pb(name, shape):
            return ctx.enter_context(nc.psum_tensor(name, shape, F32))
        psum = pb("psum", [P, 8 * 512])
        ps_a = psum[:, 0:1024]
        ps_b = psum[:, 1024:2048]
        ps_c = psum[:, 2048:3072]
        ps_d = psum[:, 3072:3584]
        ps_e = psum[:, 3584:4096]

        def n_T_ps(v):
            return psum[:, 1024 * v:1024 * v + NT * P]

        def n_self_ps(v):
            return psum[:, 2048 + 1024 * v:2048 + 1024 * v + NT * P].rearrange("p (k d) -> p k d", d=D)

        loaded = sem("loaded")
        pads_ready = sem("pads_ready")
        const_pool = sem("const_pool")
        const_ready = sem("const_ready")
        tables_ready = sem("tables_ready")
        type_psum = sem("type_psum")
        x1_set = sem("x1_set")
        prep = sem("prep")

        block = ctx.enter_context(nc.Block())

        gidx_ready = sem("gidx_ready")
        gathered_s = sem("gathered_s")
        gathered_d = sem("gathered_d")
        hT_psum_s = sem("hT_psum_s")
        hT_psum_d = sem("hT_psum_d")
        hTs_ready = sem("hTs_ready")
        hTd_ready = sem("hTd_ready")
        q_psum = sem("q_psum")
        k_psum = sem("k_psum")
        v_psum = sem("v_psum")
        q_ready = sem("q_ready")
        k_ready = sem("k_ready")
        blocks_zero = sem("blocks_zero")
        v_ready = sem("v_ready")
        s_psum = sem("s_psum")
        soft = sem("soft")
        ex_ready = sem("ex_ready")
        vT_ready = sem("vT_ready")
        m_moved = sem("m_moved")
        aT_ready = sem("aT_ready")
        a_blocked = sem("a_blocked")
        m_psum = sem("m_psum")
        m_ready = sem("m_ready")
        edge_ready = sem("edge_ready")
        parts_ready = sem("parts_ready")
        rows_psum = sem("rows_psum")
        same_ready = sem("same_ready")
        hot_ready = sem("hot_ready")
        earlier_ready = sem("earlier_ready")
        count_ready = sem("count_ready")
        moved_ready = sem("moved_ready")
        key_kept = sem("key_kept")
        sidx_ready = sem("sidx_ready")
        o_psum = sem("o_psum")
        o_ready = sem("o_ready")
        sum_psum = sem("sum_psum")
        sum_ready = sem("sum_ready")
        added = sem("added")

        class NodeSems:
            def __init__(self, name):
                self.loaded = [sem(f"{name}_loaded{u}") for u in range(4)]
                self.stats = sem(f"{name}_stats")
                self.mv = sem(f"{name}_mv")
                self.var = sem(f"{name}_var")
                self.rstd = sem(f"{name}_rstd")
                self.bias = sem(f"{name}_bias")
                self.h = sem(f"{name}_h")
                self.h_out = [sem(f"{name}_h_out{u}") for u in range(2)]

        first = NodeSems("first")
        tail_loaded = sem("tail_loaded")
        x1_out = [sem(f"x1_out{u}") for u in range(4)]
        second = NodeSems("second")
        nT_psum = sem("nT_psum")
        nT_ready = sem("nT_ready")
        nself_psum = sem("nself_psum")
        nself = sem("nself")
        nself_out = [sem(f"nself_out{u}") for u in range(2)]

        g2idx = sem("g2idx")
        gathered2 = [sem(f"gathered2_{u}") for u in range(2)]
        edge2 = sem("edge2")
        parts2 = sem("parts2")
        hot2 = sem("hot2")
        rT_psum = sem("rT_psum")
        rT_ready = sem("rT_ready")
        rows2_psum = sem("rows2_psum")
        y_psum = sem("y_psum")
        y_hot = sem("y_hot")
        y_sel = sem("y_sel")
        same2 = sem("same2")
        earlier2 = sem("earlier2")
        count2 = sem("count2")
        moved2 = sem("moved2")
        key2 = sem("key2")
        sidx2 = sem("sidx2")
        sum2_psum = sem("sum2_psum")
        sum2 = sem("sum2")
        added2 = sem("added2")

        fin_in = [sem(f"fin_in{u}") for u in range(2)]
        fin_done = sem("fin_done")
        fin_out = [sem(f"fin_out{u}") for u in range(2)]

        flat = lambda t: t[:].rearrange("p a b c -> p (a b c)")
        big = [flat(k_blk), flat(a_blk)]

        def piece(t, at, tiles):
            return t[:, at * P:(at + tiles) * P].rearrange("p (k d) -> p k d", d=D)
        n_x = [piece(big[0], NT * u, NT) for u in range(4)]
        n_h = [piece(big[1], NT * u, NT) for u in range(2)]
        n_out = [piece(big[1], NT * (2 + u), NT) for u in range(2)]
        n_T = [q_tok, v_tok]
        r_T = [hTs, hTd]
        r_edge = [edge_f, edge_f2]
        r_parts = [edge_p, edge_p2]
        r_same = [same, same_b]
        r_sel = [out_e, out_b]
        r_idx = [s_idx, s_idx_b]
        r_key = [mx[:, 0:J], den[:, 0:J]]
        r_sum = [summed, summed_b]
        r_picked = [own_sc, a_tok, q_tok, v_tok]
        f_x = [piece(big[0], J * u, J) for u in range(2)]
        f_agg = [piece(big[0], J * (2 + u), J) for u in range(2)]
        f_out = [piece(big[1], J * u, J) for u in range(2)]
        TAIL = (N - (NN - 1) * P * NT) // NT
        TAIL_ROWS = N - (NN - 1) * P * NT - TAIL * NT
        LOADS = 24
        PREP_STEPS = 35
        CONSTS = 8

        @block.sync
        def _(sp):
            def node_rows(t, n):
                return t[bass.ds(n * (P * NT), P * NT), :].rearrange("(p k) d -> p k d", k=NT)

            sp.wait_ge(pads_ready, 1)
            sp.dma_start(x1[N:N + P, :], zeros[:]).then_inc(x1_set, 16)
            sp.dma_start(x1[N + P:ROWS, :], zeros[0:ROWS - N - P, :]).then_inc(x1_set, 16)

            def load_x(n, u):
                free, copied = counts(sp, NT * (n - 3), n * 4 - 4 * u)
                if is_past(n, 4):
                    sp.wait_ge(first.h, free)
                    sp.wait_ge(x1_out[u], copied)
                if isinstance(n, int) and n == NN - 1:
                    sp.dma_start(n_x[u][TAIL:TAIL + 1, 0:TAIL_ROWS], x[N - TAIL_ROWS:N, :].rearrange(
                        "(p k) d -> p k d", p=1)).then_inc(tail_loaded, 16)
                    sp.wait_ge(tail_loaded, 16)
                    sp.dma_start(n_x[u][0:TAIL], x[n * P * NT:n * P * NT + TAIL * NT, :].rearrange(
                        "(p k) d -> p k d", k=NT)).then_inc(first.loaded[u], 16)
                else:
                    sp.dma_start(n_x[u], node_rows(x, n)).then_inc(first.loaded[u], 16)

            def store_x(n, u):
                if isinstance(n, int) and n == NN - 1:
                    sp.dma_start(x1[n * P * NT:n * P * NT + TAIL * NT, :].rearrange(
                        "(p k) d -> p k d", k=NT), n_x[u][0:TAIL]).then_inc(x1_out[u], 16)
                    sp.dma_start(x1[N - TAIL_ROWS:N, :].rearrange(
                        "(p k) d -> p k d", p=1), n_x[u][TAIL:TAIL + 1, 0:TAIL_ROWS]).then_inc(x1_out[u], 16)
                else:
                    sp.dma_start(node_rows(x1, n), n_x[u]).then_inc(x1_out[u], 16)

            def first_body(n, u):
                arrived, normal = counts(sp, (n - 2) * 4 + 16 - 4 * ((u + 2) % 4), NT * (n - 1))
                if exists(n, NN):
                    load_x(n, u)
                if exists(n - 2, NN):
                    sp.wait_ge(first.loaded[(u + 2) % 4], arrived)
                    store_x(n - 2, (u + 2) % 4)
                    sp.wait_ge(first.h, normal)
                    sp.dma_start(node_rows(h1, n - 2), n_h[u % 2]).then_inc(first.h_out[u % 2], 16)

            for n in range(4):
                first_body(n, n)
            with sp.Fori(4, NN - 7, 4) as n:
                for u in range(4):
                    first_body(n + u, u)
            for n in range(NN - 4, NN + 2):
                first_body(n, n % 4)

            def move_messages(b):
                now, = counts(sp, b + 1)
                if is_past(b, 1):
                    sp.wait_ge(o_psum, b)
                sp.wait_ge(m_ready, now)
                for j in range(J):
                    for q in range(4):
                        sp.dma_start(m_dense[DH * q:DH * (q + 1), :, j, :],
                                     m_strip[DH * j:DH * (j + 1), q::4, :]).then_inc(m_moved, 16)

            move_messages(0)
            with sp.Fori(1, NB) as b:
                move_messages(b)

            def node_body(n, u):
                free, normal, summed_up = counts(sp, NT * (n - 3), NT * (n - 1), n - 3)
                if exists(n, NN):
                    if is_past(n, 4):
                        sp.wait_ge(second.h, free)
                    sp.dma_start(n_x[u], node_rows(x1, n)).then_inc(second.loaded[u], 16)
                if exists(n - 2, NN):
                    sp.wait_ge(second.h, normal)
                    sp.dma_start(node_rows(h2, n - 2), n_h[u % 2]).then_inc(second.h_out[u % 2], 16)
                if exists(n - 4, NN):
                    sp.wait_ge(nself, summed_up)
                    sp.dma_start(node_rows(agg, n - 4), n_out[u % 2]).then_inc(nself_out[u % 2], 16)

            sp.wait_ge(added, 16 * J * NB)
            for n in range(4):
                node_body(n, n)
            with sp.Fori(4, NN - 3, 4) as n:
                for u in range(4):
                    node_body(n + u, u)
            for n in range(NN, NN + 4):
                node_body(n, n % 4)

            def fin_load(n, u, parts, first):
                if not first:
                    sp.wait_ge(fin_done, n - 1)
                sp.dma_start(f_x[u][0:parts], node_part(x1, n, parts)).then_inc(fin_in[u], 16)
                sp.dma_start(f_agg[u][0:parts], node_part(agg, n, parts)).then_inc(fin_in[u], 16)

            def node_part(t, n, parts):
                return t[bass.ds(n * (P * J), parts * J), :].rearrange("(p k) d -> p k d", k=J)

            def fin_store(n, u, parts):
                sp.wait_ge(fin_done, n + 1)
                sp.dma_start(node_part(out, n, parts), f_out[u][0:parts]).then_inc(fin_out[u], 16)

            last_parts = (N - (NB - 1) * P * J) // J
            sp.wait_ge(added2, 16 * J * NB)
            fin_load(0, 0, P, True)
            fin_load(1, 1, P, True)
            with sp.Fori(0, NB - 5, 2) as n:
                for u in range(2):
                    fin_load(n + 2 + u, u, P, False)
                    fin_store(n + u, u, P)
            fin_load(NB - 2, 0, P, False)
            fin_store(NB - 4, 0, P)
            fin_load(NB - 1, 1, last_parts, False)
            fin_store(NB - 3, 1, P)
            fin_store(NB - 2, 0, P)
            fin_store(NB - 1, 1, last_parts)
            for u in range(2):
                sp.wait_ge(fin_out[u], 16 * (NB // 2))

        @block.gpsimd
        def _(pool):
            nc.gpsimd.iota(dump[:], [[0, COLS]], base=N, channel_multiplier=1).then_inc(const_pool, 1)
            nc.gpsimd.iota(col_less_row[:], [[1, P]], base=0, channel_multiplier=-1).then_inc(const_pool, 1)
            nc.gpsimd.iota(edge_of_row[:], [[0, EG]], base=0, channel_multiplier=1).then_inc(const_pool, 1)
            nc.gpsimd.iota(edge_no[:], [[1, EG]], base=0, channel_multiplier=0).then_inc(const_pool, 1)
            nc.gpsimd.iota(rel_no[:], [[1, R]], base=0, channel_multiplier=0).then_inc(const_pool, 1)
            nc.gpsimd.iota(part_no[:], [[0, 1]], base=0, channel_multiplier=1).then_inc(const_pool, 1)
            nc.gpsimd.memset(minus_half[:], -0.5).then_inc(const_pool, 1)
            nc.gpsimd.iota(head_no[:], [[1, 4], [0, P]], base=0, channel_multiplier=0).then_inc(const_pool, 1)
            pool.wait_ge(const_pool, CONSTS)

            def node_scale(s, n, u):
                pool.wait_ge(s.var, n + 1)
                if is_past(n, 2):
                    pool.wait_ge(s.h, NT * (n - 1))
                part = slice(NT * u, NT * (u + 1))
                nc.gpsimd.tensor_tensor(rstd[:, part], var_e[:, part], minus_half[:, part], ALU.pow
                                        ).then_inc(s.rstd, 1)

            def node_scales(s):
                node_scale(s, 0, 0)
                node_scale(s, 1, 1)
                with pool.Fori(2, NN - 1, 2) as n:
                    for u in range(2):
                        node_scale(s, n + u, u)

            node_scales(first)
            pool.wait_ge(first.h, NT * NN)
            for u in range(4):
                pool.wait_ge(x1_out[u], 16 * (NN // 4) + (16 if u == 3 else 0))
            nc.gpsimd.memset(flat(k_blk), 0.0).then_inc(blocks_zero, 1)
            for u in range(2):
                pool.wait_ge(first.h_out[u], 16 * (NN // 2))
            nc.gpsimd.memset(flat(a_blk), 0.0).then_inc(blocks_zero, 1)

            def gather(b, slots):
                for s in slots:
                    nc.gpsimd.indirect_dma_start(
                        hg[:, s, :], None, h1,
                        bass.IndirectOffsetOnAxis(ap=g_idx[:, s:s + 1], axis=0)
                    ).then_inc(gathered_s if s < J else gathered_d, 16)

            def targets_may_be_gathered(b):
                now, before = counts(pool, b + 1, b)
                pool.wait_ge(const_pool, CONSTS)
                pool.wait_ge(gidx_ready, now)
                if is_past(b, 1):
                    pool.wait_ge(hT_psum_d, before)

            def sources_may_be_gathered(b):
                before, = counts(pool, b)
                pool.wait_ge(const_pool, CONSTS)
                if is_past(b, 1):
                    pool.wait_ge(hT_psum_s, before)

            def scatter(b, j):
                before, = counts(pool, 16 * (J * b + j))
                pool.wait_ge(const_pool, CONSTS)
                if is_past(b, 1) or j > 0:
                    pool.wait_ge(added, before)
                nc.gpsimd.indirect_dma_start(
                    x1, bass.IndirectOffsetOnAxis(ap=s_idx[:, j:j + 1], axis=0),
                    summed[:, j, :], None, compute_op=ALU.add).then_inc(added, 16)

            def body(i):
                add, fetch = exists(i - 2), exists(i + 2)
                if fetch:
                    targets_may_be_gathered(i + 2)
                    gather(i + 2, (J, J + 1))
                if add:
                    pool.wait_ge(sum_ready, i - 1)
                    pool.wait_ge(sidx_ready, i - 1)
                    scatter(i - 2, 0)
                if fetch:
                    gather(i + 2, (J + 2, J + 3))
                if add:
                    scatter(i - 2, 1)
                if fetch:
                    sources_may_be_gathered(i + 2)
                    gather(i + 2, (0, 1))
                if add:
                    scatter(i - 2, 2)
                if fetch:
                    gather(i + 2, (2, 3))
                if add:
                    scatter(i - 2, 3)

            for b in range(2):
                targets_may_be_gathered(b)
                gather(b, range(J, 2 * J))
                sources_may_be_gathered(b)
                gather(b, range(J))
            pool.wait_ge(x1_set, 32)
            for i in range(2):
                body(i)
            with pool.Fori(2, NB - 2) as i:
                body(i)
            for i in range(NB - 2, NB + 2):
                body(i)

            node_scales(second)

            def gather2(b, u, j):
                nc.gpsimd.indirect_dma_start(
                    hg[:, J * u + j, :], None, h2,
                    bass.IndirectOffsetOnAxis(ap=g_idx[:, J * u + j:J * u + j + 1], axis=0)
                ).then_inc(gathered2[u], 16)

            def gather2_may_start(b, u):
                now, before = counts(pool, b + 1, b - 1)
                pool.wait_ge(const_pool, CONSTS)
                pool.wait_ge(g2idx, now)
                if is_past(b, 2):
                    pool.wait_ge(rT_psum, before)

            def scatter2(b, u, j):
                before, = counts(pool, 16 * (J * b + j))
                pool.wait_ge(const_pool, CONSTS)
                if is_past(b, 1) or j > 0:
                    pool.wait_ge(added2, before)
                nc.gpsimd.indirect_dma_start(
                    agg, bass.IndirectOffsetOnAxis(ap=r_idx[u][:, j:j + 1], axis=0),
                    r_sum[u][:, j, :], None, compute_op=ALU.add).then_inc(added2, 16)

            def body2(b, u):
                pool.wait_ge(sum2, b + 1)
                pool.wait_ge(sidx2, b + 1)
                scatter2(b, u, 0)
                if exists(b + 3):
                    gather2_may_start(b + 3, 1 - u)
                    gather2(b + 3, 1 - u, 0)
                scatter2(b, u, 1)
                if exists(b + 3):
                    gather2(b + 3, 1 - u, 1)
                    gather2(b + 3, 1 - u, 2)
                scatter2(b, u, 2)
                if exists(b + 3):
                    gather2(b + 3, 1 - u, 3)
                scatter2(b, u, 3)

            for u in range(2):
                pool.wait_ge(second.h_out[u], 16 * (NN // 2))
                pool.wait_ge(nself_out[u], 16 * (NN // 2))
            for b in range(3):
                gather2_may_start(b, b % 2)
                for j in range(J):
                    gather2(b, b % 2, j)
            with pool.Fori(0, NB - 5, 2) as b:
                for u in range(2):
                    body2(b + u, u)
            for b in range(NB - 4, NB):
                body2(b, b % 2)

        @block.vector
        def _(dve):
            prep_n = [0]

            def then(ins):
                prep_n[0] += 1
                ins.then_inc(prep, 1)
                dve.wait_ge(prep, prep_n[0])

            nc.vector.memset(zeros[:], 0.0)
            dve.wait_ge(const_pool, CONSTS)
            for i in range(2):
                nc.vector.tensor_copy(raw[:, i, :], dump[:])
            then(nc.vector.memset(raw[:, 2:4, :], 0))
            nc.vector.tensor_scalar(ident_b[:], col_less_row[:], 0.0, None, ALU.is_equal)
            nc.vector.tensor_scalar(ident[:], col_less_row[:], 0.0, None, ALU.is_equal).then_inc(pads_ready, 1)
            nc.vector.tensor_scalar(lower[:], col_less_row[:], 0.0, None, ALU.is_lt)
            nc.vector.tensor_copy(part_f[:], part_no[:])
            then(nc.vector.tensor_scalar(edge_of_row[:], edge_of_row[:], EG - 1, None, ALU.bitwise_and))
            nc.vector.tensor_tensor(own_edge[:], edge_of_row[:], edge_no[:], ALU.is_equal)
            nc.vector.tensor_tensor(head_cols[:], edge_of_row[0:BR, 0:1].unsqueeze(2).to_broadcast([BR, 4, P]),
                                    head_no[0:BR], ALU.is_equal).then_inc(const_ready, 1)

            def node_moments(s, n, u):
                v = u % 2
                dve.wait_ge(s.loaded[u], 16 * (n // 4 + 1) if isinstance(n, int) else n * 4 + 16 - 4 * u)
                if is_past(n, 2):
                    dve.wait_ge(s.bias, n - 1)
                for k in range(NT):
                    nc.vector.bn_stats(stats[:, NT * v + k, :], n_x[u][:, k, :]).then_inc(s.stats, 1)
                here, = counts(dve, NT * (n + 1))
                dve.wait_ge(const_pool, CONSTS)
                dve.wait_ge(s.stats, here)
                for k in range(NT):
                    nc.vector.bn_aggr(mv[:, NT * v + k, :], stats[:, NT * v + k, :]).then_inc(s.mv, 1)
                dve.wait_ge(s.mv, NT * (n + 1))
                nc.vector.tensor_scalar(var_e[:, NT * v:NT * (v + 1)], mv[:, NT * v:NT * (v + 1), 1], EPS, None,
                                        ALU.add).then_inc(s.var, 1)

            def node_bias(s, n, v):
                dve.wait_ge(s.rstd, n + 1)
                if is_past(n, 2):
                    dve.wait_ge(s.h, NT * (n - 1))
                part = slice(NT * v, NT * (v + 1))
                nc.vector.scalar_tensor_tensor(nbias[:, part], mv[:, part, 0], -1.0, rstd[:, part],
                                               ALU.mult, ALU.mult).then_inc(s.bias, 1)

            def first_body(n, u):
                node_moments(first, n, u)
                node_bias(first, n, u % 2)

            for n in range(4):
                first_body(n, n)
            with dve.Fori(4, NN - 3, 4) as n:
                for u in range(4):
                    first_body(n + u, u)

            dve.wait_ge(loaded, 16 * LOADS)

            def by_batch(t):
                return t.rearrange("p (b j) -> p b j", j=J)
            for s in range(2):
                key = by_batch(raw[:, s, :])
                tab = (src_tab, dst_tab)[s]
                nc.vector.scalar_tensor_tensor(gather_idx[:, :, J * s:J * (s + 1)], key, float(N), key,
                                               ALU.is_lt, ALU.mult)
                nc.vector.tensor_copy(tab[:, :, 0:J], key)
                nc.vector.tensor_tensor(tab[:, :, J:2 * J], by_batch(dump[:]), key, ALU.subtract)
                then(nc.vector.tensor_copy(tab[:, :, 2 * J:3 * J], by_batch(raw[:, 2 + s, :])))
                parts = (src_parts, dst_parts)[s]
                nc.vector.tensor_copy(parts[:, :, 2 * J:3 * J], by_batch(raw[:, 2 + s, :]))
                then(nc.vector.tensor_scalar(key_bits[:], raw[:, s, :], 255, None, ALU.bitwise_and))
                nc.vector.tensor_tensor(parts[:, :, 0:J], key, by_batch(key_bits[:]), ALU.subtract)
                then(nc.vector.tensor_copy(parts[:, :, J:2 * J], by_batch(key_bits[:])))

            def masks(rows):
                n = rows // SPLIT
                row_no = part_f[0:rows]
                then(nc.vector.tensor_scalar(split_mask[0:rows, 3:4], row_no, float(n), None, ALU.is_ge))
                then(nc.vector.tensor_scalar(split_mask[0:rows, 2:3], row_no, float(2 * n), None, ALU.is_ge))
                then(nc.vector.tensor_tensor(split_mask[0:rows, 1:2], split_mask[0:rows, 3:4], split_mask[0:rows, 2:3],
                                             ALU.subtract))
                then(nc.vector.tensor_scalar(split_mask[0:rows, 0:1], row_no, float(n), None, ALU.is_lt))

            def split(full, parts, rows, part, rest):
                then(nc.vector.tensor_copy(part, full))
                then(nc.vector.tensor_scalar(parts, part, split_mask[0:rows, 0:1], None, ALU.mult))
                last = full
                for n in (1, 2):
                    then(nc.vector.tensor_tensor(rest, last, part, ALU.subtract))
                    then(nc.vector.tensor_copy(part, rest))
                    then(nc.vector.scalar_tensor_tensor(parts, part, split_mask[0:rows, n:n + 1], parts,
                                                        ALU.mult, ALU.add))
                    last = rest

            masks(BR)
            split(b_in[:], b_rows[:], BR, split_part[:], split_rest[:])
            masks(TR)
            then(nc.vector.tensor_tensor(type_of_row[:], split_mask[0:TR, 3:4], split_mask[0:TR, 2:3], ALU.add))
            then(nc.vector.scalar_tensor_tensor(type_of_row[:], type_of_row[:], -float(T3), part_f[0:TR],
                                                ALU.mult, ALU.add))
            dve.wait_ge(type_psum, 1)
            then(nc.vector.tensor_tensor(type_f[:, 0, :], ps_d[0:TR, 0:D], bo_rows[:], ALU.add))
            split(type_f[:], type_out[:], TR, split_part[0:TR, 0:1, 0:D], split_rest[0:TR, 0:1, 0:D])
            assert prep_n[0] == PREP_STEPS

            def gather_rows(b):
                if is_past(b, 1):
                    dve.wait_ge(gathered_s, 16 * J * b)
                    dve.wait_ge(gathered_d, 16 * J * b)
                nc.vector.tensor_copy(g_idx[:], gather_idx[:, bass.ds(b, 1), :].rearrange("p b j -> p (b j)")
                                      ).then_inc(gidx_ready, 1)

            def scores_first(b):
                sv = ps_a[:].rearrange("p (n e) -> p n e", e=EG)
                ov = own_sc[:].rearrange("p (n e) -> p n e", e=EG)
                own = own_edge[:].unsqueeze(1).to_broadcast([P, G * H, EG])
                dve.wait_ge(s_psum, b + 1)
                nc.vector.tensor_tensor(ov, sv, own, ALU.mult).then_inc(soft, 1)

            def softmax(b):
                ov = own_sc[:].rearrange("p (n e) -> p n e", e=EG)
                av = a_tok[:].rearrange("p (n e) -> p n e", e=EG)
                own = own_edge[:].unsqueeze(1).to_broadcast([P, G * H, EG])
                dve.wait_ge(soft, 8 * b + 1)
                nc.vector.tensor_reduce(sc[:].rearrange("p g h -> p (g h)"), ov, AX.X, ALU.add).then_inc(soft, 1)
                dve.wait_ge(soft, 8 * b + 2)
                nc.vector.tensor_reduce(mx[:], sc[:], AX.X, ALU.max).then_inc(soft, 1)
                dve.wait_ge(soft, 8 * b + 3)
                nc.vector.tensor_tensor(cen[:], sc[:], mx[:].unsqueeze(2).to_broadcast([P, G, H]), ALU.subtract
                                        ).then_inc(soft, 1)
                turn_values(b)
                if exists(b - 2):
                    scatter_rows(b - 2)
                dve.wait_ge(ex_ready, b + 1)
                nc.vector.tensor_reduce(den[:], ex[:], AX.X, ALU.add).then_inc(soft, 1)
                dve.wait_ge(soft, 8 * b + 5)
                nc.vector.reciprocal(rden[:], den[:]).then_inc(soft, 1)
                dve.wait_ge(soft, 8 * b + 6)
                nc.vector.tensor_tensor(pr[:], ex[:], rden[:].unsqueeze(2).to_broadcast([P, G, H]), ALU.mult
                                        ).then_inc(soft, 1)
                dve.wait_ge(soft, 8 * b + 7)
                nc.vector.tensor_tensor(av, pr[:].rearrange("p g h -> p (g h)").unsqueeze(2).to_broadcast([P, G * H, EG]),
                                        own, ALU.mult).then_inc(soft, 1)

            def turn_values(b):
                dve.wait_ge(v_ready, b + 1)
                if is_past(b, 1):
                    dve.wait_ge(m_psum, b)
                nc.vector.transpose(vT[:], v_tok[:]).then_inc(vT_ready, 1)

            def turn_attention(b):
                dve.wait_ge(soft, 8 * (b + 1))
                if is_past(b, 1):
                    dve.wait_ge(a_blocked, 4 * b)
                nc.vector.transpose(a_turned[:].rearrange("p n t -> p (n t)"), a_tok[:]).then_inc(aT_ready, 1)

            def stage_edges(b):
                if is_past(b, 1):
                    dve.wait_ge(rows_psum, b)
                    dve.wait_ge(key_kept, b)
                nc.vector.tensor_copy(edge_p[:], src_parts[:, bass.ds(b, 1), :].rearrange("p b j -> p (b j)")
                                      ).then_inc(parts_ready, 1)
                nc.vector.tensor_copy(edge_f[:], src_tab[:, bass.ds(b, 1), :].rearrange("p b j -> p (b j)")
                                      ).then_inc(edge_ready, 1)

            def repeats(b):
                dve.wait_ge(edge_ready, b + 1)
                dve.wait_ge(rows_psum, b + 1)
                if is_past(b, 1):
                    dve.wait_ge(sum_psum, b)
                nc.vector.tensor_tensor(same[:], ps_a[:, 0:512].rearrange("p (j e) -> p j e", j=J),
                                        edge_f[:, 0:J].unsqueeze(2).to_broadcast([P, J, P]), ALU.is_equal
                                        ).then_inc(same_ready, 1)
                if is_past(b, 1):
                    dve.wait_ge(o_psum, b)
                nc.vector.tensor_scalar(type_hot[:], ps_a[0:TR, 512:1024], type_of_row[:], None, ALU.is_equal
                                        ).then_inc(hot_ready, 1)
                dve.wait_ge(same_ready, b + 1)
                nc.vector.tensor_tensor(earlier[:], same[:], lower[:].unsqueeze(1).to_broadcast([P, J, P]), ALU.mult
                                        ).then_inc(earlier_ready, 1)
                dve.wait_ge(earlier_ready, b + 1)
                nc.vector.tensor_reduce(count[:], earlier[:], AX.X, ALU.add).then_inc(count_ready, 1)
                dve.wait_ge(count_ready, b + 1)
                nc.vector.scalar_tensor_tensor(moved[:], count[:], 0.0, edge_f[:, J:2 * J], ALU.is_gt, ALU.mult
                                               ).then_inc(moved_ready, 1)
                dve.wait_ge(moved_ready, b + 1)
                nc.vector.tensor_tensor(s_keys[:, bass.ds(b, 1), :].rearrange("p b j -> p (b j)"), moved[:],
                                        edge_f[:, 0:J], ALU.add).then_inc(key_kept, 1)

            def scatter_rows(b):
                dve.wait_ge(key_kept, b + 1)
                if is_past(b, 1):
                    dve.wait_ge(added, 16 * J * b)
                nc.vector.tensor_copy(s_idx[:], s_keys[:, bass.ds(b, 1), :].rearrange("p b j -> p (b j)")
                                      ).then_inc(sidx_ready, 1)

            def body(i):
                if exists(i - 1):
                    stage_edges(i - 1)
                if exists(i):
                    scores_first(i)
                if exists(i + 2):
                    gather_rows(i + 2)
                if exists(i):
                    softmax(i)
                elif exists(i - 2):
                    scatter_rows(i - 2)
                if exists(i):
                    turn_attention(i)
                if exists(i - 1):
                    repeats(i - 1)

            gather_rows(0)
            gather_rows(1)
            for i in range(2):
                body(i)
            with dve.Fori(2, NB - 2) as i:
                body(i)
            for i in range(NB - 2, NB + 2):
                body(i)

            def node_self(n, v):
                dve.wait_ge(nself_psum, n + 1)
                if is_past(n, 2):
                    dve.wait_ge(nself_out[v], n * 8 - 8 * v)
                nc.vector.tensor_tensor(n_out[v], n_self_ps(v), b_self[:].unsqueeze(1).to_broadcast([P, NT, D]),
                                        ALU.add).then_inc(nself, 1)

            def node_body(n, u):
                if exists(n, NN):
                    node_moments(second, n, u)
                if exists(n - 3, NN):
                    node_self(n - 3, (u + 1) % 2)
                if exists(n, NN):
                    node_bias(second, n, u % 2)

            for n in range(4):
                node_body(n, n)
            with dve.Fori(4, NN - 3, 4) as n:
                for u in range(4):
                    node_body(n + u, u)
            for n in range(NN, NN + 3):
                node_body(n, n % 4)

            def gather2_rows(b, u):
                if is_past(b, 2):
                    dve.wait_ge(gathered2[u], 16 * J * (b // 2) if isinstance(b, int) else b * 32 - 32 * u)
                nc.vector.tensor_copy(g_idx[:, J * u:J * (u + 1)],
                                      gather_idx[:, bass.ds(b, 1), 0:J].rearrange("p b j -> p (b j)")
                                      ).then_inc(g2idx, 1)

            def rel_stage(b, u):
                if is_past(b, 2):
                    dve.wait_ge(key2, b - 1)
                    dve.wait_ge(rows2_psum, b - 1)
                nc.vector.tensor_copy(r_parts[u][:], dst_parts[:, bass.ds(b, 1), :].rearrange("p b j -> p (b j)")
                                      ).then_inc(parts2, 1)
                nc.vector.tensor_copy(r_edge[u][:], dst_tab[:, bass.ds(b, 1), :].rearrange("p b j -> p (b j)")
                                      ).then_inc(edge2, 1)

            def rel_repeats(b, u):
                dve.wait_ge(edge2, b + 1)
                nc.vector.tensor_tensor(hot[u], r_edge[u][:, 2 * J:3 * J].unsqueeze(2).to_broadcast([P, J, R]),
                                        rel_no[:].unsqueeze(1).to_broadcast([P, J, R]), ALU.is_equal
                                        ).then_inc(hot2, 1)
                dve.wait_ge(rows2_psum, b + 1)
                if is_past(b, 2):
                    dve.wait_ge(sum2_psum, b - 1)
                nc.vector.tensor_tensor(r_same[u][:], ps_e[:].rearrange("p (j e) -> p j e", j=J),
                                        r_edge[u][:, 0:J].unsqueeze(2).to_broadcast([P, J, P]), ALU.is_equal
                                        ).then_inc(same2, 1)
                dve.wait_ge(same2, b + 1)
                nc.vector.tensor_tensor(earlier[:], r_same[u][:], lower[:].unsqueeze(1).to_broadcast([P, J, P]),
                                        ALU.mult).then_inc(earlier2, 1)
                dve.wait_ge(earlier2, b + 1)
                nc.vector.tensor_reduce(count[:], earlier[:], AX.X, ALU.add).then_inc(count2, 1)
                dve.wait_ge(count2, b + 1)
                nc.vector.scalar_tensor_tensor(moved[:], count[:], 0.0, r_edge[u][:, J:2 * J], ALU.is_gt, ALU.mult
                                               ).then_inc(moved2, 1)
                dve.wait_ge(moved2, b + 1)
                if is_past(b, 2):
                    dve.wait_ge(sidx2, b - 1)
                nc.vector.tensor_tensor(r_key[u], moved[:], r_edge[u][:, 0:J], ALU.add).then_inc(key2, 1)

            def rel_scatter_rows(b, u):
                dve.wait_ge(key2, b + 1)
                if is_past(b, 2):
                    dve.wait_ge(added2, 16 * J * (b - 1))
                nc.vector.tensor_copy(r_idx[u][:], r_key[u]).then_inc(sidx2, 1)

            def rel_select(b, u):
                dve.wait_ge(hot2, b + 1)

                def keep(j):
                    dve.wait_ge(y_psum, J * b + j + 1)
                    if is_past(b, 1):
                        dve.wait_ge(y_sel, J * (b - 1) + j + 1)
                    nc.vector.tensor_tensor(r_picked[j][:].rearrange("p (o r) -> p r o", r=R),
                                            (ps_a, ps_b)[j % 2][:].rearrange("p (r o) -> p r o", r=R),
                                            hot[u][:, j, :].unsqueeze(2).to_broadcast([P, R, D]), ALU.mult
                                            ).then_inc(y_hot, 1)

                def add_up(j):
                    dve.wait_ge(y_hot, J * b + j + 1)
                    if j == 0 and is_past(b, 2):
                        dve.wait_ge(sum2_psum, b - 1)
                    nc.vector.tensor_reduce(r_sel[u][:, j, :], r_picked[j][:].rearrange("p (o r) -> p o r", r=R),
                                            AX.X, ALU.add).then_inc(y_sel, 1)
                keep(0)
                if exists(b + 2):
                    gather2_rows(b + 2, u)
                for j in range(1, J):
                    keep(j)
                    add_up(j - 1)
                rel_scatter_rows(b, u)
                add_up(J - 1)

            def rel_body(b, u):
                if exists(b + 1):
                    rel_stage(b + 1, 1 - u)
                rel_select(b, u)
                if exists(b + 1):
                    rel_repeats(b + 1, 1 - u)

            hot = [cen[:, 0:J, :], ex[:, 0:J, :]]
            gather2_rows(0, 0)
            gather2_rows(1, 1)
            rel_stage(0, 0)
            rel_repeats(0, 0)
            for u in range(2):
                rel_body(u, u)
            with dve.Fori(2, NB - 3, 2) as b:
                for u in range(2):
                    rel_body(b + u, u)
            for u in range(2):
                rel_body(NB - 2 + u, u)

            def fin(n, u, parts):
                dve.wait_ge(fin_in[u], n * 16 + 32 - 16 * u)
                if is_past(n, 2):
                    dve.wait_ge(fin_out[u], n * 8 - 8 * u)
                nc.vector.scalar_tensor_tensor(f_out[u][0:parts], f_agg[u][0:parts], 0.0, f_x[u][0:parts],
                                               ALU.max, ALU.add).then_inc(fin_done, 1)

            fin(0, 0, P)
            fin(1, 1, P)
            with dve.Fori(2, NB - 3, 2) as n:
                for u in range(2):
                    fin(n + u, u, P)
            fin(NB - 2, 0, P)
            fin(NB - 1, 1, (N - (NB - 1) * P * J) // J)

        @block.scalar
        def _(act):
            act.wait_ge(pads_ready, 1)
            whole = E // COLS
            for i, t in enumerate((src, dst, et3, et8)):
                full = t[0:whole * COLS].rearrange("(p c) -> p c", c=COLS)
                act.dma_start(raw[0:112, i, :], full[0:112, :]).then_inc(loaded, 16)
                act.dma_start(raw[112:whole, i, :], full[112:whole, :]).then_inc(loaded, 16)
                act.dma_start(raw[whole:whole + 1, i, 0:E - whole * COLS],
                              t[whole * COLS:E].rearrange("(a c) -> a c", a=1)).then_inc(loaded, 16)
            act.dma_start(wq[:], wqT).then_inc(loaded, 16)
            act.dma_start(wk[:], wkT).then_inc(loaded, 16)
            act.dma_start(wv[:], wvT).then_inc(loaded, 16)
            act.dma_start(wo[:], woT.rearrange("(a p) o -> p a o", p=P)).then_inc(loaded, 16)
            act.dma_start(emb[:], embT.rearrange("(a p) t -> p a t", p=P)).then_inc(loaded, 16)
            act.dma_start(bo_rows[:], bo.rearrange("(a d) -> a d", a=1).to_broadcast([TR, D])).then_inc(loaded, 16)
            act.dma_start(w_rel[:], wrel.rearrange("r d o -> d r o")).then_inc(loaded, 16)
            act.dma_start(w_self[:], wself).then_inc(loaded, 16)
            act.dma_start(b_self[:], bias1.rearrange("(a d) -> a d", a=1).to_broadcast([P, D])).then_inc(loaded, 16)
            for n, b in enumerate((bqR, bkR, bvR)):
                act.dma_start(b_in[:, n, :], b).then_inc(loaded, 16)

            def normalise(s, n, u):
                v = u % 2
                act.wait_ge(s.bias, n + 1)
                if is_past(n, 2):
                    act.wait_ge(s.h_out[v], n * 8 - 8 * v)
                for k in range(NT):
                    nc.scalar.activation(n_h[v][:, k, :], n_x[u][:, k, :], ACT.Relu,
                                         scale=rstd[:, NT * v + k:NT * v + k + 1],
                                         bias=nbias[:, NT * v + k:NT * v + k + 1]).then_inc(s.h, 1)

            for n in range(4):
                normalise(first, n, n)
            with act.Fori(4, NN - 3, 4) as n:
                for u in range(4):
                    normalise(first, n + u, u)

            def tile_sums(b):
                act.wait_ge(sum_psum, b + 1)
                if is_past(b, 1):
                    act.wait_ge(added, 16 * J * b)
                nc.scalar.copy(summed[:].rearrange("p j d -> p (j d)"), ps_d[:]).then_inc(sum_ready, 1)

            def exponent(b):
                act.wait_ge(soft, 8 * b + 4)
                nc.scalar.activation(ex[:], cen[:], ACT.Exp, scale=SCALE).then_inc(ex_ready, 1)

            def messages(b):
                act.wait_ge(m_psum, b + 1)
                if is_past(b, 1):
                    act.wait_ge(m_moved, 256 * b)
                nc.scalar.copy(m_strip[:].rearrange("p h (g e) -> p h g e", e=EG),
                               ps_b[:].rearrange("p (g h e) -> p h g e", h=H, e=EG)).then_inc(m_ready, 1)

            def turned_targets(b):
                act.wait_ge(hT_psum_d, b + 1)
                nc.scalar.copy(hTd[:], ps_e[:]).then_inc(hTd_ready, 1)

            def turned_sources(b):
                act.wait_ge(hT_psum_s, b + 1)
                nc.scalar.copy(hTs[:], ps_d[:]).then_inc(hTs_ready, 1)

            def attention_blocks(b):
                act.wait_ge(aT_ready, b + 1)
                if is_past(b, 1):
                    act.wait_ge(m_psum, b)
                for c in range(4):
                    s = slice(TOK * c, TOK * (c + 1))
                    nc.scalar.copy(a_blk[s, :, c, :], a_turned[s]).then_inc(a_blocked, 1)

            def by_group(t):
                return t[:].rearrange("p (n h e) -> p n h e", h=H, e=EG)

            def by_head(t):
                return t.rearrange("p (h n e) -> p n h e", h=H, e=EG)

            def keys_and_queries(b):
                act.wait_ge(k_psum, b + 1)

                def keys(j):
                    s = slice(DH * j, DH * (j + 1))
                    nc.scalar.copy(k_blk[s, :, j, :].rearrange("p n (h e) -> p n h e", h=H), by_head(ps_b[s, :])
                                   ).then_inc(k_ready, 1)
                for j in range(J - 1):
                    keys(j)
                act.wait_ge(q_psum, b + 1)
                nc.scalar.copy(by_group(q_tok), by_head(ps_c[:])).then_inc(q_ready, 1)
                keys(J - 1)

            def values(b):
                act.wait_ge(v_psum, b + 1)
                if is_past(b, 1):
                    act.wait_ge(vT_ready, b)
                nc.scalar.copy(by_group(v_tok), by_head(ps_c[:])).then_inc(v_ready, 1)

            def edge_out(b):
                act.wait_ge(o_psum, b + 1)
                if is_past(b, 1):
                    act.wait_ge(sum_psum, b)
                nc.scalar.copy(out_e[:].rearrange("p j d -> p (j d)"), ps_d[:]).then_inc(o_ready, 1)

            def body(i):
                if exists(i - 1):
                    attention_blocks(i - 1)
                if exists(i - 2):
                    edge_out(i - 2)
                if exists(i):
                    exponent(i)
                if exists(i - 1):
                    messages(i - 1)
                if exists(i + 1):
                    turned_targets(i + 1)
                if exists(i - 2):
                    tile_sums(i - 2)
                if exists(i + 1):
                    turned_sources(i + 1)
                    keys_and_queries(i + 1)
                    values(i + 1)

            act.wait_ge(blocks_zero, 2)
            act.wait_ge(loaded, 16 * LOADS)
            turned_targets(0)
            turned_sources(0)
            keys_and_queries(0)
            values(0)
            for i in range(2):
                body(i)
            with act.Fori(2, NB - 1) as i:
                body(i)
            for i in range(NB - 1, NB + 2):
                body(i)

            def node_body(n, u):
                v = u % 2
                if exists(n, NN):
                    if is_past(n, 2):
                        act.wait_ge(nT_psum, n - 1)
                    normalise(second, n, u)
                if exists(n - 1, NN):
                    act.wait_ge(nT_psum, n)
                    if is_past(n, 3):
                        act.wait_ge(nself_psum, n - 2)
                    nc.scalar.copy(n_T[1 - v][:, 0:NT * P], n_T_ps(1 - v)).then_inc(nT_ready, 1)

            for n in range(4):
                node_body(n, n)
            with act.Fori(4, NN - 3, 4) as n:
                for u in range(4):
                    node_body(n + u, u)
            node_body(NN, 0)

            def rel_turned(b, u):
                act.wait_ge(rT_psum, b + 1)
                if is_past(b, 2):
                    act.wait_ge(y_psum, J * (b - 1))
                nc.scalar.copy(r_T[u][:], ps_d[:]).then_inc(rT_ready, 1)

            def rel_sums(b, u):
                act.wait_ge(sum2_psum, b + 1)
                if is_past(b, 2):
                    act.wait_ge(added2, 16 * J * (b - 1))
                nc.scalar.copy(r_sum[u][:].rearrange("p j d -> p (j d)"), ps_c[:, 0:512]).then_inc(sum2, 1)

            def rel_body(b, u):
                if exists(b - 1):
                    rel_sums(b - 1, 1 - u)
                if exists(b + 1):
                    rel_turned(b + 1, 1 - u)

            rel_turned(0, 0)
            for u in range(2):
                rel_body(u, u)
            with act.Fori(2, NB - 3, 2) as b:
                for u in range(2):
                    rel_body(b + u, u)
            for b in range(NB - 2, NB + 1):
                rel_body(b, b % 2)

        @block.tensor
        def _(pe):
            pe.wait_ge(loaded, 16 * LOADS)
            pe.wait_ge(const_ready, 1)
            for a in range(2):
                last = nc.tensor.matmul(ps_d[0:TR, 0:D], emb[:, a, :], wo[:, a, :], start=(a == 0), stop=(a == 1))
            last.then_inc(type_psum, 1)
            pe.wait_ge(prep, PREP_STEPS)

            def turn_targets(b):
                pe.wait_ge(gathered_d, 16 * J * (b + 1))
                if is_past(b, 1):
                    pe.wait_ge(hTd_ready, b)
                for j in range(J):
                    last = nc.tensor.transpose(ps_e[:, P * j:P * (j + 1)], hg[:, J + j, :], ident[:])
                last.then_inc(hT_psum_d, 1)

            def turn_sources(b):
                pe.wait_ge(gathered_s, 16 * J * (b + 1))
                if is_past(b, 3):
                    pe.wait_ge(sum_ready, b - 2)
                elif is_past(b, 1):
                    pe.wait_ge(hTs_ready, b)
                for j in range(J):
                    last = nc.tensor.transpose(ps_d[:, P * j:P * (j + 1)], hg[:, j, :], ident[:])
                last.then_inc(hT_psum_s, 1)

            def projection(dest, n, w, cols, done=None, halves=(0, 1)):
                for half in halves:
                    bank = slice(512 * half, 512 * (half + 1))
                    nc.tensor.matmul(dest[:, bank], b_rows[:, n, P * half:P * (half + 1)],
                                     head_cols[:].rearrange("p h c -> p (h c)"), start=True, stop=False)
                    for h in range(4 * half, 4 * half + 4):
                        for s in range(4):
                            last = nc.tensor.matmul(dest[DH * s:DH * (s + 1), P * h:P * (h + 1)],
                                                    w[:, DH * h:DH * (h + 1)], cols(s),
                                                    start=False, stop=(h % 4 == 3))
                if done is not None:
                    last.then_inc(done, 1)

            def keys(b):
                pe.wait_ge(hTd_ready, b + 1)
                if is_past(b, 2):
                    pe.wait_ge(m_ready, b - 1)
                projection(ps_b, 1, wk, lambda j: hTd[:, P * j:P * (j + 1)], halves=(0,))
                turn_sources(b)
                projection(ps_b, 1, wk, lambda j: hTd[:, P * j:P * (j + 1)], k_psum, halves=(1,))

            def queries(b):
                pe.wait_ge(hTs_ready, b + 1)
                if is_past(b, 1):
                    pe.wait_ge(v_ready, b)
                projection(ps_c, 0, wq, lambda j: hTs[:, P * j:P * (j + 1)], q_psum)

            def values(b):
                turned = hTd[:].rearrange("d (j n c e) -> d c n j e", j=J, c=4, e=EG)
                pe.wait_ge(q_ready, b + 1)
                projection(ps_c, 2, wv, lambda c: turned[:, c], v_psum)

            def scores(b):
                now, before = counts(pe, b + 1, b - 1)
                all_k, = counts(pe, J * (b + 1))
                pe.wait_ge(const_ready, 1)
                pe.wait_ge(k_ready, all_k)
                pe.wait_ge(q_ready, now)
                if is_past(b, 2):
                    pe.wait_ge(hot_ready, before)
                for g in range(G):
                    c = g % 4
                    last = nc.tensor.matmul(ps_a[TOK * c:TOK * (c + 1), P * (g // 4):P * (g // 4 + 1)],
                                            q_tok[:, TOK * g:TOK * (g + 1)],
                                            k_blk[:, g].rearrange("p j t -> p (j t)"), start=True, stop=True)
                last.then_inc(s_psum, 1)

            def messages(b):
                turned_all, now = counts(pe, 4 * (b + 1), b + 1)
                pe.wait_ge(const_ready, 1)
                pe.wait_ge(a_blocked, turned_all)
                pe.wait_ge(vT_ready, now)
                for n in range(G):
                    g8, j = n // J, n % J
                    last = nc.tensor.matmul(ps_b[DH * j:DH * (j + 1), P * g8:P * (g8 + 1)],
                                            vT[:, TOK * n:TOK * (n + 1)],
                                            a_blk[:, n].rearrange("p c t -> p (c t)"), start=True, stop=True)
                last.then_inc(m_psum, 1)

            def key_rows(dest, parts, j):
                for k in range(2):
                    last = nc.tensor.matmul(dest, parts[:, J * k + j:J * k + j + 1].to_broadcast([P, P]), ident_b[:],
                                            start=(k == 0), stop=(k == 1))
                return last

            def rows(b):
                pe.wait_ge(parts_ready, b + 1)
                if exists(b + 1):
                    pe.wait_ge(soft, 8 * (b + 1) + 1)
                elif is_past(b, 1):
                    pe.wait_ge(hot_ready, b)
                for j in range(J):
                    key_rows(ps_a[:, P * j:P * (j + 1)], edge_p, j)
                    last = nc.tensor.matmul(ps_a[:, 512 + P * j:512 + P * (j + 1)],
                                            edge_p[:, 2 * J + j:2 * J + j + 1].to_broadcast([P, P]), ident_b[:],
                                            start=True, stop=True)
                last.then_inc(rows_psum, 1)

            def edge_out(b):
                pe.wait_ge(m_moved, 256 * (b + 1))
                pe.wait_ge(hot_ready, b + 1)
                if exists(b + 2):
                    pe.wait_ge(hTs_ready, b + 3)
                else:
                    pe.wait_ge(sum_ready, b)
                for j in range(J):
                    o = ps_d[:, P * j:P * (j + 1)]
                    nc.tensor.matmul(o, m_dense[:, 0, j, :], wo[:, 0, :], start=True, stop=False)
                    nc.tensor.matmul(o, m_dense[:, 1, j, :], wo[:, 1, :], start=False, stop=False)
                    last = nc.tensor.matmul(o, type_hot[:, P * j:P * (j + 1)], type_out[:, 0],
                                            start=False, stop=True)
                last.then_inc(o_psum, 1)

            def tile_sums(b):
                pe.wait_ge(o_ready, b + 1)
                pe.wait_ge(same_ready, b + 1)
                for j in range(J):
                    last = nc.tensor.matmul(ps_d[:, P * j:P * (j + 1)], same[:, j, :], out_e[:, j, :],
                                            start=True, stop=True)
                last.then_inc(sum_psum, 1)

            def body(i):
                if exists(i):
                    scores(i)
                if exists(i - 2):
                    edge_out(i - 2)
                if exists(i - 1):
                    messages(i - 1)
                if exists(i + 1):
                    turn_targets(i + 1)
                if exists(i - 2):
                    tile_sums(i - 2)
                if exists(i + 1):
                    keys(i + 1)
                    queries(i + 1)
                if exists(i - 1):
                    rows(i - 1)
                if exists(i + 1):
                    values(i + 1)

            turn_targets(0)
            keys(0)
            queries(0)
            values(0)
            for i in range(2):
                body(i)
            with pe.Fori(2, NB - 1) as i:
                body(i)
            for i in range(NB - 1, NB + 2):
                body(i)

            def node_body(n, u):
                v = u % 2
                if exists(n, NN):
                    pe.wait_ge(second.h, NT * (n + 1))
                    if is_past(n, 2):
                        pe.wait_ge(nT_ready, n - 1)
                    for k in range(NT):
                        last = nc.tensor.transpose(n_T_ps(v)[:, P * k:P * (k + 1)], n_h[v][:, k, :], ident[:])
                    last.then_inc(nT_psum, 1)
                if exists(n - 1, NN):
                    pe.wait_ge(nT_ready, n)
                    if is_past(n, 3):
                        pe.wait_ge(nself, n - 2)
                    for k in range(NT):
                        last = nc.tensor.matmul(n_self_ps(1 - v)[:, k, :], n_T[1 - v][:, P * k:P * (k + 1)], w_self[:],
                                                start=True, stop=True)
                    last.then_inc(nself_psum, 1)

            for n in range(4):
                node_body(n, n)
            with pe.Fori(4, NN - 3, 4) as n:
                for u in range(4):
                    node_body(n + u, u)
            node_body(NN, 0)

            def rel_turn(b, u):
                pe.wait_ge(gathered2[u], 16 * J * (b // 2 + 1) if isinstance(b, int) else b * 32 + 64 - 32 * u)
                if is_past(b, 1):
                    pe.wait_ge(rT_ready, b)
                for j in range(J):
                    last = nc.tensor.transpose(ps_d[:, P * j:P * (j + 1)], hg[:, J * u + j, :], ident[:])
                last.then_inc(rT_psum, 1)

            def rel_rows(b, u):
                pe.wait_ge(parts2, b + 1)
                if is_past(b, 1):
                    pe.wait_ge(same2, b)
                for j in range(J):
                    last = key_rows(ps_e[:, P * j:P * (j + 1)], r_parts[u], j)
                last.then_inc(rows2_psum, 1)

            def rel_products(b, u, js):
                if 0 in js:
                    pe.wait_ge(rT_ready, b + 1)
                for j in js:
                    if is_past(b, 1) or j >= 2:
                        pe.wait_ge(y_hot, J * b + j - 1)
                    y = (ps_a, ps_b)[j % 2]
                    for a in range(2):
                        last = nc.tensor.matmul(y[:, 512 * a:512 * (a + 1)], r_T[u][:, P * j:P * (j + 1)],
                                                w_rel[:, 4 * a:4 * (a + 1), :].rearrange("p r o -> p (r o)"),
                                                start=True, stop=True)
                    last.then_inc(y_psum, 1)

            def rel_sums(b, u):
                pe.wait_ge(y_sel, J * (b + 1))
                pe.wait_ge(same2, b + 1)
                if is_past(b, 1):
                    pe.wait_ge(sum2, b)
                for j in range(J):
                    last = nc.tensor.matmul(ps_c[:, P * j:P * (j + 1)], r_same[u][:, j, :], r_sel[u][:, j, :],
                                            start=True, stop=True)
                last.then_inc(sum2_psum, 1)

            def rel_body(b, u):
                if exists(b):
                    rel_products(b, u, (0, 1))
                if exists(b - 1):
                    rel_sums(b - 1, 1 - u)
                if exists(b):
                    rel_products(b, u, (2, 3))
                if exists(b + 1):
                    rel_rows(b + 1, 1 - u)
                    rel_turn(b + 1, 1 - u)

            rel_rows(0, 0)
            rel_turn(0, 0)
            for u in range(2):
                rel_body(u, u)
            with pe.Fori(2, NB - 3, 2) as b:
                for u in range(2):
                    rel_body(b + u, u)
            for b in range(NB - 2, NB + 1):
                rel_body(b, b % 2)


def kernel(**inputs):
    import numpy as np
    import concourse.bacc as bacc
    from concourse import mybir as mb
    from concourse.bass_utils import run_bass_kernel_spmd

    def turned(name):
        return np.ascontiguousarray(np.asarray(inputs[name]).T)

    def by_head(name):
        b = np.asarray(inputs[name]).reshape(2, 4, DH)
        return np.ascontiguousarray(np.tile(np.tile(b, (1, 1, 4)).transpose(1, 0, 2).reshape(4, 2 * P), (SPLIT, 1)))

    def plain(name):
        return np.ascontiguousarray(inputs[name])

    given = {
        "x": plain("x"), "src": plain("src"), "dst": plain("dst"),
        "et3": plain("edge_type_3"), "et8": plain("edge_type_8"),
        "wqT": turned("L0_gnn_Wq"), "bqR": by_head("L0_gnn_bq"),
        "wkT": turned("L0_gnn_Wk"), "bkR": by_head("L0_gnn_bk"),
        "wvT": turned("L0_gnn_Wv"), "bvR": by_head("L0_gnn_bv"),
        "embT": np.ascontiguousarray(np.tile(turned("L0_gnn_edge_emb"), (1, SPLIT))), "woT": turned("L0_gnn_Wo"), "bo": plain("L0_gnn_bo"),
        "wrel": plain("L1_gnn_weight"), "wself": plain("L1_gnn_self_loop_weight"), "bias1": plain("L1_gnn_bias"),
    }
    nc = bacc.Bacc("TRN2", target_bir_lowering=False, num_devices=1)
    aps = {k: nc.dram_tensor(f"in_{k}", a.shape, mb.dt.from_np(a.dtype), kind="ExternalInput").ap()
           for k, a in given.items()}
    out = nc.dram_tensor("out", (N, D), mb.dt.float32, kind="ExternalOutput").ap()
    build(nc, *aps.values(), out)
    r = run_bass_kernel_spmd(nc, [{f"in_{k}": a for k, a in given.items()}], core_ids=[0])
    return r.results[0]["out"]
```

```python
import concourse.bass as bass
from concourse import mybir
from contextlib import ExitStack

F32 = mybir.dt.float32
I32 = mybir.dt.int32
ALU = mybir.AluOpType
ACT = mybir.ActivationFunctionType
AX = mybir.AxisListType

P = 128
D = 128
H = 8
DH = 32
HID = H * DH
N = 50000
E = 50000
T3 = 3
R = 8
J = 4
BF16 = mybir.dt.bfloat16
NT = 7
NB = -(-E // (P * J))
COLS = NB * J
ROWS = NB * P * J
EG = 4
G = P // EG
TOK = EG * H
NN = ROWS // (P * NT)
SPLIT = 3
EPS = 1e-5
SCALE = float(DH) ** -0.5


def is_past(b, k):
    return not isinstance(b, int) or b >= k


def exists(b, n=NB):
    return not isinstance(b, int) or 0 <= b < n


def counts(eng, *values):
    return [v if isinstance(v, int) else eng.to_reg(v) for v in values]


def build(nc, x, src, dst, et3, et8, wqT, bqC, wkT, bkR, wvT, bvC, embT, woT, bo, wrel, wself, bias1, out):
    x1 = nc.dram_tensor("x1", (ROWS, D), F32, kind="Internal").ap()
    h1 = nc.dram_tensor("h1", (ROWS, D), F32, kind="Internal").ap()
    h2 = nc.dram_tensor("h2", (ROWS, D), F32, kind="Internal").ap()
    agg = nc.dram_tensor("agg", (ROWS, D), F32, kind="Internal").ap()
    agg_odd = nc.dram_tensor("agg_odd", (ROWS, D), F32, kind="Internal").ap()

    ctx = ExitStack()
    with ctx:
        def sb(name, shape, dt=F32):
            return ctx.enter_context(nc.sbuf_tensor(name, shape, dt))

        def sem(name):
            return ctx.enter_context(nc.semaphore(name))

        ident = sb("ident", [P, P])
        lower = sb("lower", [P, P])
        col_less_row = sb("col_less_row", [P, P], I32)
        ident_b = sb("ident_b", [P, P], BF16)
        own_edge = sb("own_edge", [P, EG])
        edge_of_row = sb("edge_of_row", [P, EG], I32)
        edge_no = sb("edge_no", [P, EG], I32)
        rel_no = sb("rel_no", [P, R], I32)
        part_no = sb("part_no", [P, 1], I32)
        part_f = sb("part_f", [P, 1])
        minus_half = sb("minus_half", [P, 2 * NT])
        zeros = sb("zeros", [P, D])
        wq = sb("wq", [P, HID])
        wk = sb("wk", [P, HID])
        wv = sb("wv", [P, HID])
        wo = sb("wo", [P, 2, D])
        emb = sb("emb", [P, 2, SPLIT * T3])
        BR = SPLIT * 4
        b_in = sb("b_in", [BR, 1, 2 * P])
        b_rows = sb("b_rows", [BR, 1, 2 * P], BF16)
        bq_cols = sb("bq_cols", [P, H])
        bv_cols = sb("bv_cols", [P, H])
        head_cols = sb("head_cols", [BR, 4, P], BF16)
        head_no = sb("head_no", [P, 4, P], I32)
        TR = SPLIT * T3
        bo_rows = sb("bo_rows", [TR, D])
        type_f = sb("type_f", [TR, 1, D])
        type_out = sb("type_out", [TR, 1, D], BF16)
        split_part = sb("split_part", [BR, 1, 2 * P], BF16)
        split_rest = sb("split_rest", [BR, 1, 2 * P])
        split_mask = sb("split_mask", [BR, SPLIT + 1])
        type_of_row = sb("type_of_row", [TR, 1])
        w_rel = sb("w_rel", [P, R, D])
        w_self = sb("w_self", [P, D])
        b_self = sb("b_self", [P, D])

        raw = sb("raw", [P, 4, COLS], I32)
        gather_idx = sb("gather_idx", [P, NB, 2 * J], I32)
        dump = sb("dump", [P, COLS], I32)
        src_tab = sb("src_tab", [P, NB, 3 * J])
        dst_tab = sb("dst_tab", [P, NB, 3 * J])
        src_parts = sb("src_parts", [P, NB, 3 * J], BF16)
        dst_parts = sb("dst_parts", [P, NB, 3 * J], BF16)
        key_bits = sb("key_bits", [P, COLS], I32)

        g_idx = sb("g_idx", [P, 2 * J], I32)
        stats = sb("stats", [P, 2 * NT, 6])
        mv = sb("mv", [P, 2 * NT, 2])
        var_e = sb("var_e", [P, 2 * NT])
        rstd = sb("rstd", [P, 2 * NT])
        nbias = sb("nbias", [P, 2 * NT])
        hg = sb("hg", [P, 2 * J, D])
        hTs = sb("hTs", [P, J * P])
        hTd = sb("hTd", [P, J * P])
        q_tok = sb("q_tok", [P, G * TOK])
        k_blk = sb("k_blk", [P, G, J, TOK])
        v_tok = sb("v_tok", [P, G * TOK])
        own_sc = sb("own_sc", [P, G * TOK])
        sc = sb("sc", [P, G, H])
        mx = sb("mx", [P, G])
        cen = sb("cen", [P, G, H])
        ex = sb("ex", [P, G, H])
        den = sb("den", [P, G])
        rden = sb("rden", [P, G])
        pr = sb("pr", [P, G, H])
        a_tok = sb("a_tok", [P, G * TOK])
        a_turned = sb("a_turned", [P, G, TOK])
        a_blk = sb("a_blk", [P, G, 4, TOK])
        vT = sb("vT", [P, G * TOK])
        m_strip = sb("m_strip", [P, H, P])
        m_dense = sb("m_dense", [P, 2, J, P])
        summed_b = sb("summed_b", [P, J, D])
        odd_b = sb("odd_b", [P, 2 * J, D])
        out_b = sb("out_b", [P, J, D])
        edge_f = sb("edge_f", [P, 3 * J])
        edge_f2 = sb("edge_f2", [P, 3 * J])
        edge_p = sb("edge_p", [P, 3 * J], BF16)
        edge_p2 = sb("edge_p2", [P, 3 * J], BF16)
        same = sb("same", [P, J, P])
        same_b = sb("same_b", [P, J, P])
        earlier = sb("earlier", [P, J, P])
        count = sb("count", [P, J])
        moved = sb("moved", [P, J])
        s_keys = sb("s_keys", [P, NB, J])
        s_idx = sb("s_idx", [P, J], I32)
        s_idx_b = sb("s_idx_b", [P, J], I32)
        type_hot = sb("type_hot", [TR, J * P], BF16)
        out_e = sb("out_e", [P, J, D])
        summed = sb("summed", [P, J, D])

        def pb(name, shape):
            return ctx.enter_context(nc.psum_tensor(name, shape, F32))
        psum = pb("psum", [P, 8 * 512])
        ps_a = psum[:, 0:1024]
        ps_b = psum[:, 1024:2048]
        ps_c = psum[:, 2048:3072]
        ps_d = psum[:, 3072:3584]
        ps_e = psum[:, 3584:4096]

        def n_T_ps(v):
            return psum[:, 1024 * v:1024 * v + NT * P]

        def n_self_ps(v):
            return psum[:, 2048 + 1024 * v:2048 + 1024 * v + NT * P].rearrange("p (k d) -> p k d", d=D)

        loaded = sem("loaded")
        pads_ready = sem("pads_ready")
        const_pool = sem("const_pool")
        const_ready = sem("const_ready")
        type_psum = sem("type_psum")
        x1_set = sem("x1_set")
        prep = sem("prep")

        block = ctx.enter_context(nc.Block())

        gidx_ready = sem("gidx_ready")
        gathered_s = sem("gathered_s")
        gathered_d = sem("gathered_d")
        hT_psum_s = sem("hT_psum_s")
        hT_psum_d = sem("hT_psum_d")
        hTs_ready = sem("hTs_ready")
        hTd_ready = sem("hTd_ready")
        q_psum = sem("q_psum")
        k_psum = sem("k_psum")
        v_psum = sem("v_psum")
        q_ready = sem("q_ready")
        k_ready = sem("k_ready")
        blocks_zero = sem("blocks_zero")
        v_ready = sem("v_ready")
        s_psum = sem("s_psum")
        soft = sem("soft")
        ex_ready = sem("ex_ready")
        vT_ready = sem("vT_ready")
        m_moved = sem("m_moved")
        aT_ready = sem("aT_ready")
        a_blocked = sem("a_blocked")
        m_psum = sem("m_psum")
        m_ready = sem("m_ready")
        edge_ready = sem("edge_ready")
        parts_ready = sem("parts_ready")
        rows_psum = sem("rows_psum")
        same_ready = sem("same_ready")
        hot_ready = sem("hot_ready")
        earlier_ready = sem("earlier_ready")
        count_ready = sem("count_ready")
        moved_ready = sem("moved_ready")
        key_kept = sem("key_kept")
        sidx_ready = sem("sidx_ready")
        o_psum = sem("o_psum")
        o_ready = sem("o_ready")
        sum_psum = sem("sum_psum")
        sum_ready = sem("sum_ready")
        added = sem("added")

        class NodeSems:
            def __init__(self, name):
                self.loaded = [sem(f"{name}_loaded{u}") for u in range(8)]
                self.stats = sem(f"{name}_stats")
                self.mv = sem(f"{name}_mv")
                self.var = sem(f"{name}_var")
                self.rstd = sem(f"{name}_rstd")
                self.bias = sem(f"{name}_bias")
                self.h = sem(f"{name}_h")
                self.h_out = [sem(f"{name}_h_out{u}") for u in range(4)]

        first = NodeSems("first")
        tail_loaded = sem("tail_loaded")
        x1_out = [sem(f"x1_out{u}") for u in range(8)]
        second = NodeSems("second")

        g2idx = sem("g2idx")
        gathered2 = [sem(f"gathered2_{u}") for u in range(2)]
        edge2 = sem("edge2")
        parts2 = sem("parts2")
        hot2 = sem("hot2")
        rT_psum = sem("rT_psum")
        rT_ready = sem("rT_ready")
        rows2_psum = sem("rows2_psum")
        y_psum = sem("y_psum")
        masked_even = sem("masked_even")
        masked_even_b = sem("masked_even_b")
        masked_odd = sem("masked_odd")
        selected = sem("selected")
        sum2_psum = sem("sum2_psum")
        same2 = sem("same2")
        earlier2 = sem("earlier2")
        count2 = sem("count2")
        moved2 = sem("moved2")
        key2 = sem("key2")
        sidx2 = sem("sidx2")
        sum2 = sem("sum2")
        sums_set = sem("sums_set")
        added2 = [sem("added2_even"), sem("added2_odd")]

        third = NodeSems("third")
        nT_psum = sem("nT_psum")
        nT_ready = sem("nT_ready")
        nself_psum = sem("nself_psum")
        pair_in = [sem(f"pair_in{u}") for u in range(4)]
        pair_sum = sem("pair_sum")
        self_added = sem("self_added")
        out_ready = sem("out_ready")
        out_stored = [sem(f"out_stored{u}") for u in range(4)]

        flat = lambda t: t[:].rearrange("p a b c -> p (a b c)")
        big = [flat(k_blk), flat(a_blk)]

        def piece(t, at, tiles):
            return t[:, at * P:(at + tiles) * P].rearrange("p (k d) -> p k d", d=D)
        n_x = [piece(t, NT * u, NT) for t in big for u in range(4)]
        three_d = lambda t: t[:].rearrange("p a b -> p (a b)")
        l_h = [piece(three_d(m_strip), 0, NT), piece(flat(m_dense), 0, NT)]
        n_h = l_sum = [piece(t, 0, NT) for t in (own_sc, a_tok, vT, three_d(a_turned))]
        l_odd = [piece(three_d(t), 0, NT) for t in (hg, odd_b)]
        n_T = [q_tok, v_tok]
        hot = [cen[:, 0:J, :], ex[:, 0:J, :]]
        r_T = [hTs, hTd]
        r_edge = [edge_f, edge_f2]
        r_parts = [edge_p, edge_p2]
        r_sel = [out_e, out_b]
        r_same = [same, same_b]
        r_idx = [s_idx, s_idx_b]
        r_key = [mx[:, 0:J], den[:, 0:J]]
        r_sum = [summed, summed_b]
        r_picked = [own_sc, a_tok, q_tok, v_tok]
        TAIL = (N - (NN - 1) * P * NT) // NT
        TAIL_ROWS = N - (NN - 1) * P * NT - TAIL * NT
        LOADS = 24
        PREP_STEPS = 35
        CONSTS = 8

        @block.sync
        def _(sp):
            def node_rows(t, n):
                return t[bass.ds(n * (P * NT), P * NT), :].rearrange("(p k) d -> p k d", k=NT)

            sp.wait_ge(pads_ready, 1)
            sp.dma_start(x1[N:N + P, :], zeros[:]).then_inc(x1_set, 16)
            sp.dma_start(x1[N + P:ROWS, :], zeros[0:ROWS - N - P, :]).then_inc(x1_set, 16)

            def load_x(n, u):
                free, copied = counts(sp, NT * (n - 7), n * 2 - 2 * u)
                if is_past(n, 8):
                    sp.wait_ge(first.h, free)
                    sp.wait_ge(x1_out[u], copied)
                if isinstance(n, int) and n == NN - 1:
                    sp.dma_start(n_x[u][TAIL:TAIL + 1, 0:TAIL_ROWS], x[N - TAIL_ROWS:N, :].rearrange(
                        "(p k) d -> p k d", p=1)).then_inc(tail_loaded, 16)
                    sp.wait_ge(tail_loaded, 16)
                    sp.dma_start(n_x[u][0:TAIL], x[n * P * NT:n * P * NT + TAIL * NT, :].rearrange(
                        "(p k) d -> p k d", k=NT)).then_inc(first.loaded[u], 16)
                else:
                    sp.dma_start(n_x[u], node_rows(x, n)).then_inc(first.loaded[u], 16)

            def store_x(n, u):
                if isinstance(n, int) and n == NN - 1:
                    sp.dma_start(x1[n * P * NT:n * P * NT + TAIL * NT, :].rearrange(
                        "(p k) d -> p k d", k=NT), n_x[u][0:TAIL]).then_inc(x1_out[u], 16)
                    sp.dma_start(x1[N - TAIL_ROWS:N, :].rearrange(
                        "(p k) d -> p k d", p=1), n_x[u][TAIL:TAIL + 1, 0:TAIL_ROWS]).then_inc(x1_out[u], 16)
                else:
                    sp.dma_start(node_rows(x1, n), n_x[u]).then_inc(x1_out[u], 16)

            def first_body(n, u):
                x_u, h_u = (u + 4) % 8, (u + 3) % 4
                arrived, normal = counts(sp, (n - 4) * 2 + 16 - 2 * x_u, NT * (n - 4))
                if exists(n, NN):
                    load_x(n, u)
                if exists(n - 4, NN):
                    sp.wait_ge(first.loaded[x_u], arrived)
                    store_x(n - 4, x_u)
                if exists(n - 5, NN):
                    sp.wait_ge(first.h, normal)
                    sp.dma_start(node_rows(h1, n - 5), n_h[h_u]).then_inc(first.h_out[h_u], 16)

            for n in range(8):
                first_body(n, n)
            with sp.Fori(8, NN - 15, 8) as n:
                for u in range(8):
                    first_body(n + u, u)
            for n in range(NN - 8, NN + 5):
                first_body(n, n % 8)

            def move_messages(b):
                now, = counts(sp, 2 * (b + 1))
                if is_past(b, 1):
                    sp.wait_ge(o_psum, b)
                sp.wait_ge(m_ready, now)
                for j in range(J):
                    for q in range(4):
                        sp.dma_start(m_dense[DH * q:DH * (q + 1), :, j, :],
                                     m_strip[DH * j:DH * (j + 1), q::4, :]).then_inc(m_moved, 16)
                for t, start in ((agg, b_self), (agg_odd, zeros)):
                    sp.dma_start(t[bass.ds(b * (P * J), P * J), :].rearrange("(p k) d -> p k d", k=J),
                                 start[:].unsqueeze(1).to_broadcast([P, J, D])).then_inc(sums_set, 16)

            sp.wait_ge(loaded, 16 * LOADS)
            move_messages(0)
            with sp.Fori(1, NB) as b:
                move_messages(b)

            def second_body(n, u):
                h_u = (u + 3) % 4
                free, normal = counts(sp, NT * (n - 7), NT * (n - 4))
                if exists(n, NN):
                    if is_past(n, 8):
                        sp.wait_ge(second.h, free)
                    sp.dma_start(n_x[u], node_rows(x1, n)).then_inc(second.loaded[u], 16)
                if exists(n - 5, NN):
                    sp.wait_ge(second.h, normal)
                    sp.dma_start(node_rows(h2, n - 5), n_h[h_u]).then_inc(second.h_out[h_u], 16)

            sp.wait_ge(added, 16 * J * NB)
            for n in range(8):
                second_body(n, n)
            with sp.Fori(8, NN - 7, 8) as n:
                for u in range(8):
                    second_body(n + u, u)
            for n in range(NN, NN + 5):
                second_body(n, n % 8)

            def last_store(n, u):
                if isinstance(n, int) and n == NN - 1:
                    sp.dma_start(out[n * P * NT:n * P * NT + TAIL * NT, :].rearrange(
                        "(p k) d -> p k d", k=NT), l_sum[u][0:TAIL]).then_inc(out_stored[u], 16)
                    sp.dma_start(out[N - TAIL_ROWS:N, :].rearrange(
                        "(p k) d -> p k d", p=1), l_sum[u][TAIL:TAIL + 1, 0:TAIL_ROWS]).then_inc(out_stored[u], 16)
                else:
                    sp.dma_start(node_rows(out, n), l_sum[u]).then_inc(out_stored[u], 16)

            def last_body(n, u):
                s = (u + 1) % 4
                free, stored, paired, ready = counts(sp, n - 7, (n - 3) * 4 - 4 * s, n - 4, n - 4)
                if exists(n, NN):
                    if is_past(n, 8):
                        sp.wait_ge(out_ready, free)
                    sp.dma_start(n_x[u], node_rows(x1, n)).then_inc(third.loaded[u], 16)
                if exists(n - 3, NN):
                    if is_past(n, 7):
                        sp.wait_ge(out_stored[s], stored)
                    if is_past(n, 5):
                        sp.wait_ge(pair_sum, paired)
                    sp.dma_start(l_sum[s], node_rows(agg, n - 3)).then_inc(pair_in[s], 16)
                    sp.dma_start(l_odd[(u + 1) % 2], node_rows(agg_odd, n - 3)).then_inc(pair_in[s], 16)
                if exists(n - 5, NN):
                    sp.wait_ge(out_ready, ready)
                    last_store(n - 5, (u + 3) % 4)

            for t in range(2):
                sp.wait_ge(added2[t], 8 * J * NB)
            for n in range(8):
                last_body(n, n)
            with sp.Fori(8, NN - 15, 8) as n:
                for u in range(8):
                    last_body(n + u, u)
            for n in range(NN - 8, NN + 5):
                last_body(n, n % 8)
            for u in range(4):
                sp.wait_ge(out_stored[u], 16 * (NN // 4) + (16 if u == (NN - 1) % 4 else 0))

        @block.gpsimd
        def _(pool):
            nc.gpsimd.iota(dump[:], [[0, COLS]], base=N, channel_multiplier=1).then_inc(const_pool, 1)
            nc.gpsimd.iota(col_less_row[:], [[1, P]], base=0, channel_multiplier=-1).then_inc(const_pool, 1)
            nc.gpsimd.iota(edge_of_row[:], [[0, EG]], base=0, channel_multiplier=1).then_inc(const_pool, 1)
            nc.gpsimd.iota(edge_no[:], [[1, EG]], base=0, channel_multiplier=0).then_inc(const_pool, 1)
            nc.gpsimd.iota(rel_no[:], [[1, R]], base=0, channel_multiplier=0).then_inc(const_pool, 1)
            nc.gpsimd.iota(part_no[:], [[0, 1]], base=0, channel_multiplier=1).then_inc(const_pool, 1)
            nc.gpsimd.memset(minus_half[:], -0.5).then_inc(const_pool, 1)
            nc.gpsimd.iota(head_no[:], [[1, 4], [0, P]], base=0, channel_multiplier=0).then_inc(const_pool, 1)
            pool.wait_ge(const_pool, CONSTS)

            def node_scale(s, n, u):
                pool.wait_ge(s.var, n + 1)
                if is_past(n, 2):
                    pool.wait_ge(s.h, NT * (n - 1))
                part = slice(NT * u, NT * (u + 1))
                nc.gpsimd.tensor_tensor(rstd[:, part], var_e[:, part], minus_half[:, part], ALU.pow
                                        ).then_inc(s.rstd, 1)

            def node_scales(s):
                node_scale(s, 0, 0)
                node_scale(s, 1, 1)
                with pool.Fori(2, NN - 1, 2) as n:
                    for u in range(2):
                        node_scale(s, n + u, u)

            node_scales(first)
            pool.wait_ge(first.h, NT * NN)
            for u in range(8):
                pool.wait_ge(x1_out[u], 16 * (NN // 8) + (16 if u == (NN - 1) % 8 else 0))
            nc.gpsimd.memset(flat(k_blk), 0.0).then_inc(blocks_zero, 1)
            for u in range(4):
                pool.wait_ge(first.h_out[u], 16 * (NN // 4))
            nc.gpsimd.memset(flat(a_blk), 0.0).then_inc(blocks_zero, 1)

            def gather(b, slots):
                for s in slots:
                    nc.gpsimd.indirect_dma_start(
                        hg[:, s, :], None, h1,
                        bass.IndirectOffsetOnAxis(ap=g_idx[:, s:s + 1], axis=0)
                    ).then_inc(gathered_s if s < J else gathered_d, 16)

            def targets_may_be_gathered(b):
                now, before = counts(pool, b + 1, b)
                pool.wait_ge(const_pool, CONSTS)
                pool.wait_ge(gidx_ready, now)
                if is_past(b, 1):
                    pool.wait_ge(hT_psum_d, before)

            def sources_may_be_gathered(b):
                before, = counts(pool, b)
                pool.wait_ge(const_pool, CONSTS)
                if is_past(b, 1):
                    pool.wait_ge(hT_psum_s, before)

            def scatter(b, j):
                before, = counts(pool, 16 * (J * b + j))
                pool.wait_ge(const_pool, CONSTS)
                if is_past(b, 1) or j > 0:
                    pool.wait_ge(added, before)
                nc.gpsimd.indirect_dma_start(
                    x1, bass.IndirectOffsetOnAxis(ap=s_idx[:, j:j + 1], axis=0),
                    summed[:, j, :], None, compute_op=ALU.add).then_inc(added, 16)

            def body(i):
                add, fetch = exists(i - 2), exists(i + 2)
                if fetch:
                    targets_may_be_gathered(i + 2)
                    gather(i + 2, range(J, 2 * J))
                if add:
                    pool.wait_ge(sum_ready, i - 1)
                    pool.wait_ge(sidx_ready, i - 1)
                    scatter(i - 2, 0)
                if fetch:
                    sources_may_be_gathered(i + 2)
                    gather(i + 2, (0, 1))
                if add:
                    scatter(i - 2, 1)
                if fetch:
                    gather(i + 2, (2, 3))
                if add:
                    scatter(i - 2, 2)
                    scatter(i - 2, 3)

            for b in range(2):
                targets_may_be_gathered(b)
                gather(b, range(J, 2 * J))
                sources_may_be_gathered(b)
                gather(b, range(J))
            pool.wait_ge(x1_set, 32)
            for i in range(2):
                body(i)
            with pool.Fori(2, NB - 2) as i:
                body(i)
            for i in range(NB - 2, NB + 2):
                body(i)

            node_scales(second)

            def gather2(b, u, j):
                nc.gpsimd.indirect_dma_start(
                    hg[:, J * u + j, :], None, h2,
                    bass.IndirectOffsetOnAxis(ap=g_idx[:, J * u + j:J * u + j + 1], axis=0)
                ).then_inc(gathered2[u], 16)

            def gather2_may_start(b, u):
                now, before = counts(pool, b + 1, b - 1)
                pool.wait_ge(const_pool, CONSTS)
                pool.wait_ge(g2idx, now)
                if is_past(b, 2):
                    pool.wait_ge(rT_psum, before)

            def scatter2(b, u, j):
                before, = counts(pool, 8 * J * b + 16 * (j // 2))
                pool.wait_ge(const_pool, CONSTS)
                if is_past(b, 1) or j > 1:
                    pool.wait_ge(added2[j % 2], before)
                nc.gpsimd.indirect_dma_start(
                    (agg, agg_odd)[j % 2], bass.IndirectOffsetOnAxis(ap=r_idx[u][:, j:j + 1], axis=0),
                    r_sum[u][:, j, :], None, compute_op=ALU.add).then_inc(added2[j % 2], 16)

            def body2(b, u):
                if exists(b + 3):
                    gather2_may_start(b + 3, 1 - u)
                    gather2(b + 3, 1 - u, 0)
                    gather2(b + 3, 1 - u, 1)
                pool.wait_ge(sum2, b + 1)
                pool.wait_ge(sidx2, b + 1)
                scatter2(b, u, 0)
                scatter2(b, u, 1)
                if exists(b + 3):
                    gather2(b + 3, 1 - u, 2)
                    gather2(b + 3, 1 - u, 3)
                scatter2(b, u, 2)
                scatter2(b, u, 3)

            pool.wait_ge(sums_set, 16 * 2 * NB)
            for u in range(4):
                pool.wait_ge(second.h_out[u], 16 * (NN // 4))
            for b in range(3):
                gather2_may_start(b, b % 2)
                for j in range(J):
                    gather2(b, b % 2, j)
            with pool.Fori(0, NB - 5, 2) as b:
                for u in range(2):
                    body2(b + u, u)
            for b in range(NB - 4, NB):
                body2(b, b % 2)

            def add_pair(n, u):
                pool.wait_ge(pair_in[u], n * 8 + 32 - 8 * u)
                nc.gpsimd.tensor_tensor(l_sum[u], l_sum[u], l_odd[u % 2], ALU.add).then_inc(pair_sum, 1)

            def last_body(n, u):
                if exists(n, NN):
                    node_scale(third, n, u % 2)
                if exists(n - 3, NN):
                    add_pair(n - 3, (u + 1) % 4)

            for n in range(4):
                last_body(n, n)
            with pool.Fori(4, NN - 3, 4) as n:
                for u in range(4):
                    last_body(n + u, u)
            for n in range(NN, NN + 3):
                last_body(n, n % 4)

        @block.vector
        def _(dve):
            prep_n = [0]

            def then(ins):
                prep_n[0] += 1
                ins.then_inc(prep, 1)
                dve.wait_ge(prep, prep_n[0])

            nc.vector.memset(zeros[:], 0.0)
            dve.wait_ge(const_pool, CONSTS)
            for i in range(2):
                nc.vector.tensor_copy(raw[:, i, :], dump[:])
            then(nc.vector.memset(raw[:, 2:4, :], 0))
            nc.vector.tensor_scalar(ident_b[:], col_less_row[:], 0.0, None, ALU.is_equal)
            nc.vector.tensor_scalar(ident[:], col_less_row[:], 0.0, None, ALU.is_equal).then_inc(pads_ready, 1)
            nc.vector.tensor_scalar(lower[:], col_less_row[:], 0.0, None, ALU.is_lt)
            nc.vector.tensor_copy(part_f[:], part_no[:])
            then(nc.vector.tensor_scalar(edge_of_row[:], edge_of_row[:], EG - 1, None, ALU.bitwise_and))
            nc.vector.tensor_tensor(own_edge[:], edge_of_row[:], edge_no[:], ALU.is_equal)
            nc.vector.tensor_tensor(head_cols[:], edge_of_row[0:BR, 0:1].unsqueeze(2).to_broadcast([BR, 4, P]),
                                    head_no[0:BR], ALU.is_equal).then_inc(const_ready, 1)

            def node_moments(s, n, u):
                v = u % 2
                dve.wait_ge(s.loaded[u], n * 2 + 16 - 2 * u)
                if is_past(n, 2):
                    dve.wait_ge(s.bias, n - 1)
                for k in range(NT):
                    nc.vector.bn_stats(stats[:, NT * v + k, :], n_x[u][:, k, :]).then_inc(s.stats, 1)
                here, = counts(dve, NT * (n + 1))
                dve.wait_ge(const_pool, CONSTS)
                dve.wait_ge(s.stats, here)
                for k in range(NT):
                    nc.vector.bn_aggr(mv[:, NT * v + k, :], stats[:, NT * v + k, :]).then_inc(s.mv, 1)
                dve.wait_ge(s.mv, NT * (n + 1))
                nc.vector.tensor_scalar(var_e[:, NT * v:NT * (v + 1)], mv[:, NT * v:NT * (v + 1), 1], EPS, None,
                                        ALU.add).then_inc(s.var, 1)

            def node_bias(s, n, v):
                dve.wait_ge(s.rstd, n + 1)
                if is_past(n, 2):
                    dve.wait_ge(s.h, NT * (n - 1))
                part = slice(NT * v, NT * (v + 1))
                nc.vector.scalar_tensor_tensor(nbias[:, part], mv[:, part, 0], -1.0, rstd[:, part],
                                               ALU.mult, ALU.mult).then_inc(s.bias, 1)

            def node_body(s, n, u):
                if exists(n, NN):
                    node_moments(s, n, u)
                if exists(n - 1, NN):
                    node_bias(s, n - 1, (u + 1) % 2)

            def node_pass(s):
                for n in range(8):
                    node_body(s, n, n)
                with dve.Fori(8, NN - 7, 8) as n:
                    for u in range(8):
                        node_body(s, n + u, u)
                node_body(s, NN, 0)

            node_pass(first)

            dve.wait_ge(loaded, 16 * LOADS)

            def by_batch(t):
                return t.rearrange("p (b j) -> p b j", j=J)
            for s in range(2):
                key = by_batch(raw[:, s, :])
                tab = (src_tab, dst_tab)[s]
                nc.vector.scalar_tensor_tensor(gather_idx[:, :, J * s:J * (s + 1)], key, float(N), key,
                                               ALU.is_lt, ALU.mult)
                nc.vector.tensor_copy(tab[:, :, 0:J], key)
                nc.vector.tensor_tensor(tab[:, :, J:2 * J], by_batch(dump[:]), key, ALU.subtract)
                then(nc.vector.tensor_copy(tab[:, :, 2 * J:3 * J], by_batch(raw[:, 2 + s, :])))
                parts = (src_parts, dst_parts)[s]
                nc.vector.tensor_copy(parts[:, :, 2 * J:3 * J], by_batch(raw[:, 2 + s, :]))
                then(nc.vector.tensor_scalar(key_bits[:], raw[:, s, :], 255, None, ALU.bitwise_and))
                nc.vector.tensor_tensor(parts[:, :, 0:J], key, by_batch(key_bits[:]), ALU.subtract)
                then(nc.vector.tensor_copy(parts[:, :, J:2 * J], by_batch(key_bits[:])))

            def masks(rows):
                n = rows // SPLIT
                row_no = part_f[0:rows]
                then(nc.vector.tensor_scalar(split_mask[0:rows, 3:4], row_no, float(n), None, ALU.is_ge))
                then(nc.vector.tensor_scalar(split_mask[0:rows, 2:3], row_no, float(2 * n), None, ALU.is_ge))
                then(nc.vector.tensor_tensor(split_mask[0:rows, 1:2], split_mask[0:rows, 3:4], split_mask[0:rows, 2:3],
                                             ALU.subtract))
                then(nc.vector.tensor_scalar(split_mask[0:rows, 0:1], row_no, float(n), None, ALU.is_lt))

            def split(full, parts, rows, part, rest):
                then(nc.vector.tensor_copy(part, full))
                then(nc.vector.tensor_scalar(parts, part, split_mask[0:rows, 0:1], None, ALU.mult))
                last = full
                for n in (1, 2):
                    then(nc.vector.tensor_tensor(rest, last, part, ALU.subtract))
                    then(nc.vector.tensor_copy(part, rest))
                    then(nc.vector.scalar_tensor_tensor(parts, part, split_mask[0:rows, n:n + 1], parts,
                                                        ALU.mult, ALU.add))
                    last = rest

            masks(BR)
            split(b_in[:], b_rows[:], BR, split_part[:], split_rest[:])
            masks(TR)
            then(nc.vector.tensor_tensor(type_of_row[:], split_mask[0:TR, 3:4], split_mask[0:TR, 2:3], ALU.add))
            then(nc.vector.scalar_tensor_tensor(type_of_row[:], type_of_row[:], -float(T3), part_f[0:TR],
                                                ALU.mult, ALU.add))
            dve.wait_ge(type_psum, 1)
            then(nc.vector.tensor_tensor(type_f[:, 0, :], ps_d[0:TR, 0:D], bo_rows[:], ALU.add))
            split(type_f[:], type_out[:], TR, split_part[0:TR, 0:1, 0:D], split_rest[0:TR, 0:1, 0:D])
            assert prep_n[0] == PREP_STEPS

            def gather_rows(b):
                if is_past(b, 1):
                    dve.wait_ge(gathered_s, 16 * J * b)
                    dve.wait_ge(gathered_d, 16 * J * b)
                nc.vector.tensor_copy(g_idx[:], gather_idx[:, bass.ds(b, 1), :].rearrange("p b j -> p (b j)")
                                      ).then_inc(gidx_ready, 1)

            def scores_first(b):
                sv = ps_a[:].rearrange("p (n e) -> p n e", e=EG)
                ov = own_sc[:].rearrange("p (n e) -> p n e", e=EG)
                own = own_edge[:].unsqueeze(1).to_broadcast([P, G * H, EG])
                dve.wait_ge(s_psum, b + 1)
                nc.vector.tensor_tensor(ov, sv, own, ALU.mult).then_inc(soft, 1)

            def softmax(b):
                ov = own_sc[:].rearrange("p (n e) -> p n e", e=EG)
                av = a_tok[:].rearrange("p (n e) -> p n e", e=EG)
                own = own_edge[:].unsqueeze(1).to_broadcast([P, G * H, EG])
                dve.wait_ge(soft, 8 * b + 1)
                nc.vector.tensor_reduce(sc[:].rearrange("p g h -> p (g h)"), ov, AX.X, ALU.add).then_inc(soft, 1)
                dve.wait_ge(soft, 8 * b + 2)
                nc.vector.tensor_reduce(mx[:], sc[:], AX.X, ALU.max).then_inc(soft, 1)
                dve.wait_ge(soft, 8 * b + 3)
                nc.vector.tensor_tensor(cen[:], sc[:], mx[:].unsqueeze(2).to_broadcast([P, G, H]), ALU.subtract
                                        ).then_inc(soft, 1)
                turn_values(b)
                if exists(b - 2):
                    scatter_rows(b - 2)
                dve.wait_ge(ex_ready, b + 1)
                nc.vector.tensor_reduce(den[:], ex[:], AX.X, ALU.add).then_inc(soft, 1)
                dve.wait_ge(soft, 8 * b + 5)
                nc.vector.reciprocal(rden[:], den[:]).then_inc(soft, 1)
                dve.wait_ge(soft, 8 * b + 6)
                nc.vector.tensor_tensor(pr[:], ex[:], rden[:].unsqueeze(2).to_broadcast([P, G, H]), ALU.mult
                                        ).then_inc(soft, 1)
                dve.wait_ge(soft, 8 * b + 7)
                nc.vector.tensor_tensor(av, pr[:].rearrange("p g h -> p (g h)").unsqueeze(2).to_broadcast([P, G * H, EG]),
                                        own, ALU.mult).then_inc(soft, 1)

            def queries(b):
                dve.wait_ge(q_psum, b + 1)
                for half in range(2):
                    hs = slice(4 * half, 4 * half + 4)
                    nc.vector.tensor_tensor(q_tok[:].rearrange("p (n h e) -> p n h e", h=H, e=EG)[:, :, hs],
                                            ps_c[:].rearrange("p (h n e) -> p n h e", h=H, e=EG)[:, :, hs],
                                            bq_cols[:, hs].unsqueeze(1).unsqueeze(3).to_broadcast([P, G, 4, EG]),
                                            ALU.add).then_inc(q_ready, 1)

            def turn_values(b):
                dve.wait_ge(v_ready, b + 1)
                if is_past(b, 1):
                    dve.wait_ge(m_psum, b)
                nc.vector.transpose(vT[:], v_tok[:]).then_inc(vT_ready, 1)

            def turn_attention(b):
                dve.wait_ge(soft, 8 * (b + 1))
                if is_past(b, 1):
                    dve.wait_ge(a_blocked, 4 * b)
                nc.vector.transpose(a_turned[:].rearrange("p n t -> p (n t)"), a_tok[:]).then_inc(aT_ready, 1)

            def stage_edges(b):
                if is_past(b, 1):
                    dve.wait_ge(rows_psum, b)
                    dve.wait_ge(key_kept, b)
                nc.vector.tensor_copy(edge_p[:], src_parts[:, bass.ds(b, 1), :].rearrange("p b j -> p (b j)")
                                      ).then_inc(parts_ready, 1)
                nc.vector.tensor_copy(edge_f[:], src_tab[:, bass.ds(b, 1), :].rearrange("p b j -> p (b j)")
                                      ).then_inc(edge_ready, 1)

            def repeats(b):
                dve.wait_ge(edge_ready, b + 1)
                dve.wait_ge(rows_psum, b + 1)
                if is_past(b, 1):
                    dve.wait_ge(sum_psum, b)
                nc.vector.tensor_tensor(same[:], ps_a[:, 0:512].rearrange("p (j e) -> p j e", j=J),
                                        edge_f[:, 0:J].unsqueeze(2).to_broadcast([P, J, P]), ALU.is_equal
                                        ).then_inc(same_ready, 1)
                if is_past(b, 1):
                    dve.wait_ge(o_psum, b)
                nc.vector.tensor_scalar(type_hot[:], ps_a[0:TR, 512:1024], type_of_row[:], None, ALU.is_equal
                                        ).then_inc(hot_ready, 1)
                dve.wait_ge(same_ready, b + 1)
                nc.vector.tensor_tensor(earlier[:], same[:], lower[:].unsqueeze(1).to_broadcast([P, J, P]), ALU.mult
                                        ).then_inc(earlier_ready, 1)
                dve.wait_ge(earlier_ready, b + 1)
                nc.vector.tensor_reduce(count[:], earlier[:], AX.X, ALU.add).then_inc(count_ready, 1)
                dve.wait_ge(count_ready, b + 1)
                nc.vector.scalar_tensor_tensor(moved[:], count[:], 0.0, edge_f[:, J:2 * J], ALU.is_gt, ALU.mult
                                               ).then_inc(moved_ready, 1)
                dve.wait_ge(moved_ready, b + 1)
                nc.vector.tensor_tensor(s_keys[:, bass.ds(b, 1), :].rearrange("p b j -> p (b j)"), moved[:],
                                        edge_f[:, 0:J], ALU.add).then_inc(key_kept, 1)

            def scatter_rows(b):
                dve.wait_ge(key_kept, b + 1)
                if is_past(b, 1):
                    dve.wait_ge(added, 16 * J * b)
                nc.vector.tensor_copy(s_idx[:], s_keys[:, bass.ds(b, 1), :].rearrange("p b j -> p (b j)")
                                      ).then_inc(sidx_ready, 1)

            def body(i):
                if exists(i - 1):
                    stage_edges(i - 1)
                if exists(i):
                    scores_first(i)
                if exists(i + 2):
                    gather_rows(i + 2)
                if exists(i):
                    softmax(i)
                elif exists(i - 2):
                    scatter_rows(i - 2)
                if exists(i):
                    turn_attention(i)
                if exists(i + 1):
                    queries(i + 1)
                if exists(i - 1):
                    repeats(i - 1)

            gather_rows(0)
            gather_rows(1)
            queries(0)
            for i in range(2):
                body(i)
            with dve.Fori(2, NB - 2) as i:
                body(i)
            for i in range(NB - 2, NB + 2):
                body(i)

            node_pass(second)

            def gather2_rows(b, u):
                if is_past(b, 2):
                    dve.wait_ge(gathered2[u], 16 * J * (b // 2) if isinstance(b, int) else b * 32 - 32 * u)
                nc.vector.tensor_copy(g_idx[:, J * u:J * (u + 1)],
                                      gather_idx[:, bass.ds(b, 1), 0:J].rearrange("p b j -> p (b j)")
                                      ).then_inc(g2idx, 1)

            def rel_stage(b, u):
                if is_past(b, 2):
                    dve.wait_ge(key2, b - 1)
                    dve.wait_ge(rows2_psum, b - 1)
                nc.vector.tensor_copy(r_parts[u][:], dst_parts[:, bass.ds(b, 1), :].rearrange("p b j -> p (b j)")
                                      ).then_inc(parts2, 1)
                nc.vector.tensor_copy(r_edge[u][:], dst_tab[:, bass.ds(b, 1), :].rearrange("p b j -> p (b j)")
                                      ).then_inc(edge2, 1)

            def rel_repeats(b, u):
                dve.wait_ge(edge2, b + 1)
                if is_past(b, 2):
                    dve.wait_ge(sum2_psum, b - 1)
                nc.vector.tensor_tensor(hot[u], r_edge[u][:, 2 * J:3 * J].unsqueeze(2).to_broadcast([P, J, R]),
                                        rel_no[:].unsqueeze(1).to_broadcast([P, J, R]), ALU.is_equal
                                        ).then_inc(hot2, 1)
                dve.wait_ge(rows2_psum, b + 1)
                nc.vector.tensor_tensor(r_same[u][:], ps_e[:].rearrange("p (j e) -> p j e", j=J),
                                        r_edge[u][:, 0:J].unsqueeze(2).to_broadcast([P, J, P]), ALU.is_equal
                                        ).then_inc(same2, 1)
                dve.wait_ge(same2, b + 1)
                nc.vector.tensor_tensor(earlier[:], r_same[u][:], lower[:].unsqueeze(1).to_broadcast([P, J, P]),
                                        ALU.mult).then_inc(earlier2, 1)
                dve.wait_ge(earlier2, b + 1)
                nc.vector.tensor_reduce(count[:], earlier[:], AX.X, ALU.add).then_inc(count2, 1)
                dve.wait_ge(count2, b + 1)
                nc.vector.scalar_tensor_tensor(moved[:], count[:], 0.0, r_edge[u][:, J:2 * J], ALU.is_gt, ALU.mult
                                               ).then_inc(moved2, 1)
                dve.wait_ge(moved2, b + 1)
                if is_past(b, 2):
                    dve.wait_ge(sidx2, b - 1)
                nc.vector.tensor_tensor(r_key[u], moved[:], r_edge[u][:, 0:J], ALU.add).then_inc(key2, 1)

            def rel_scatter_rows(b, u):
                dve.wait_ge(key2, b + 1)
                if is_past(b, 2):
                    for t in range(2):
                        dve.wait_ge(added2[t], 8 * J * (b - 1))
                nc.vector.tensor_copy(r_idx[u][:], r_key[u]).then_inc(sidx2, 1)

            def rel_mask(b, u, j):
                dve.wait_ge(hot2, b + 1)
                dve.wait_ge(y_psum, J * b + j + 1)
                if is_past(b, 1):
                    dve.wait_ge(selected, J * (b - 1) + j + 1)
                rels = slice(0, R // 2)
                nc.vector.tensor_tensor(r_picked[j][:].rearrange("p (o r) -> p r o", r=R)[:, rels],
                                        ps_a[:].rearrange("p (r o) -> p r o", r=R)[:, rels],
                                        hot[u][:, j, rels].unsqueeze(2).to_broadcast([P, R // 2, D]), ALU.mult
                                        ).then_inc(masked_even, 1)

            def rel_add_up(b, u, j):
                dve.wait_ge((masked_even, masked_odd)[j % 2], J // 2 * b + j // 2 + 1)
                if j % 2 == 0:
                    dve.wait_ge(masked_even_b, J // 2 * b + j // 2 + 1)
                if j == 0 and is_past(b, 2):
                    dve.wait_ge(sum2_psum, b - 1)
                nc.vector.tensor_reduce(r_sel[u][:, j, :], r_picked[j][:].rearrange("p (o r) -> p o r", r=R),
                                        AX.X, ALU.add).then_inc(selected, 1)

            def rel_body(b, u):
                if exists(b):
                    rel_mask(b, u, 0)
                if exists(b - 1):
                    rel_add_up(b - 1, 1 - u, 3)
                if exists(b + 1):
                    rel_stage(b + 1, 1 - u)
                if exists(b):
                    rel_add_up(b, u, 0)
                    rel_mask(b, u, 2)
                if exists(b + 3):
                    gather2_rows(b + 3, 1 - u)
                if exists(b):
                    rel_add_up(b, u, 1)
                    rel_scatter_rows(b, u)
                    rel_add_up(b, u, 2)
                if exists(b + 1):
                    rel_repeats(b + 1, 1 - u)

            gather2_rows(0, 0)
            gather2_rows(1, 1)
            gather2_rows(2, 0)
            rel_stage(0, 0)
            rel_repeats(0, 0)
            for u in range(2):
                rel_body(u, u)
            with dve.Fori(2, NB - 5, 2) as b:
                for u in range(2):
                    rel_body(b + u, u)
            for b in range(NB - 4, NB + 1):
                rel_body(b, b % 2)

            def finish(n, u):
                r = l_sum[u % 4]
                dve.wait_ge(pair_sum, n + 1)
                dve.wait_ge(nself_psum, n + 1)
                nc.vector.tensor_tensor(r, n_self_ps(u % 2), r, ALU.add).then_inc(self_added, 1)
                dve.wait_ge(self_added, n + 1)
                nc.vector.scalar_tensor_tensor(r, r, 0.0, n_x[u], ALU.max, ALU.add).then_inc(out_ready, 1)

            def last_body(n, u):
                node_body(third, n, u)
                if exists(n - 4, NN):
                    finish(n - 4, (u + 4) % 8)

            for n in range(8):
                last_body(n, n)
            with dve.Fori(8, NN - 7, 8) as n:
                for u in range(8):
                    last_body(n + u, u)
            for n in range(NN, NN + 4):
                last_body(n, n % 8)

        @block.scalar
        def _(act):
            act.wait_ge(pads_ready, 1)
            whole = E // COLS
            for i, t in enumerate((src, dst, et3, et8)):
                full = t[0:whole * COLS].rearrange("(p c) -> p c", c=COLS)
                act.dma_start(raw[0:112, i, :], full[0:112, :]).then_inc(loaded, 16)
                act.dma_start(raw[112:whole, i, :], full[112:whole, :]).then_inc(loaded, 16)
                act.dma_start(raw[whole:whole + 1, i, 0:E - whole * COLS],
                              t[whole * COLS:E].rearrange("(a c) -> a c", a=1)).then_inc(loaded, 16)
            act.dma_start(wq[:], wqT).then_inc(loaded, 16)
            act.dma_start(wk[:], wkT).then_inc(loaded, 16)
            act.dma_start(wv[:], wvT).then_inc(loaded, 16)
            act.dma_start(wo[:], woT.rearrange("(a p) o -> p a o", p=P)).then_inc(loaded, 16)
            act.dma_start(emb[:], embT.rearrange("(a p) t -> p a t", p=P)).then_inc(loaded, 16)
            act.dma_start(bo_rows[:], bo.rearrange("(a d) -> a d", a=1).to_broadcast([TR, D])).then_inc(loaded, 16)
            act.dma_start(w_rel[:], wrel.rearrange("r d o -> d r o")).then_inc(loaded, 16)
            act.dma_start(w_self[:], wself).then_inc(loaded, 16)
            act.dma_start(b_self[:], bias1.rearrange("(a d) -> a d", a=1).to_broadcast([P, D])).then_inc(loaded, 16)
            act.dma_start(b_in[:, 0, :], bkR).then_inc(loaded, 16)
            act.dma_start(bq_cols[:], bqC).then_inc(loaded, 16)
            act.dma_start(bv_cols[:], bvC).then_inc(loaded, 16)

            def normalise(s, n, u, h):
                v = u % 2
                act.wait_ge(s.bias, n + 1)
                for k in range(NT):
                    nc.scalar.activation(h[:, k, :], n_x[u][:, k, :], ACT.Relu,
                                         scale=rstd[:, NT * v + k:NT * v + k + 1],
                                         bias=nbias[:, NT * v + k:NT * v + k + 1]).then_inc(s.h, 1)

            def node_body(s, n, u):
                v = u % 4
                if is_past(n, 4):
                    act.wait_ge(s.h_out[v], n * 4 - 4 * v)
                normalise(s, n, u, n_h[v])

            def node_pass(s):
                for n in range(8):
                    node_body(s, n, n)
                with act.Fori(8, NN - 7, 8) as n:
                    for u in range(8):
                        node_body(s, n + u, u)

            node_pass(first)

            def tile_sums(b):
                act.wait_ge(sum_psum, b + 1)
                if is_past(b, 1):
                    act.wait_ge(added, 16 * J * b)
                nc.scalar.copy(summed[:].rearrange("p j d -> p (j d)"), ps_a[:, 0:512]).then_inc(sum_ready, 1)

            def exponent(b):
                act.wait_ge(soft, 8 * b + 4)
                nc.scalar.activation(ex[:], cen[:], ACT.Exp, scale=SCALE).then_inc(ex_ready, 1)

            def messages(b):
                act.wait_ge(m_psum, b + 1)
                if is_past(b, 1):
                    act.wait_ge(m_moved, 256 * b)
                for half in range(2):
                    gs = slice(G // 2 * half, G // 2 * (half + 1))
                    nc.scalar.copy(m_strip[:].rearrange("p h (g e) -> p h g e", e=EG)[:, :, gs],
                                   ps_b[:].rearrange("p (g h e) -> p h g e", h=H, e=EG)[:, :, gs]
                                   ).then_inc(m_ready, 1)

            def turned_targets(b):
                act.wait_ge(hT_psum_d, b + 1)
                nc.scalar.copy(hTd[:], ps_e[:]).then_inc(hTd_ready, 1)

            def turned_sources(b):
                act.wait_ge(hT_psum_s, b + 1)
                nc.scalar.copy(hTs[:], ps_d[:]).then_inc(hTs_ready, 1)

            def attention_blocks(b):
                act.wait_ge(aT_ready, b + 1)
                if is_past(b, 1):
                    act.wait_ge(m_psum, b)
                for c in range(4):
                    s = slice(TOK * c, TOK * (c + 1))
                    nc.scalar.copy(a_blk[s, :, c, :], a_turned[s]).then_inc(a_blocked, 1)

            def by_group(t):
                return t[:].rearrange("p (n h e) -> p n h e", h=H, e=EG)

            def by_head(t):
                return t.rearrange("p (h n e) -> p n h e", h=H, e=EG)

            def keys_by_block(b):
                act.wait_ge(k_psum, b + 1)

                for j in range(J):
                    s = slice(DH * j, DH * (j + 1))
                    nc.scalar.copy(k_blk[s, :, j, :].rearrange("p n (h e) -> p n h e", h=H), by_head(ps_b[s, :])
                                   ).then_inc(k_ready, 1)

            def values(b):
                act.wait_ge(v_psum, b + 1)
                if is_past(b, 1):
                    act.wait_ge(vT_ready, b)
                for h in range(H):
                    last = nc.scalar.activation(by_group(v_tok)[:, :, h], by_head(ps_c[:])[:, :, h], ACT.Identity,
                                                bias=bv_cols[:, h:h + 1])
                last.then_inc(v_ready, 1)

            def edge_out(b):
                act.wait_ge(o_psum, b + 1)
                if is_past(b, 1):
                    act.wait_ge(sum_psum, b)
                nc.scalar.copy(out_e[:].rearrange("p j d -> p (j d)"), ps_d[:]).then_inc(o_ready, 1)

            def body(i):
                if exists(i + 1):
                    turned_targets(i + 1)
                if exists(i - 1):
                    messages(i - 1)
                if exists(i):
                    exponent(i)
                if exists(i - 2):
                    edge_out(i - 2)
                if exists(i + 1):
                    turned_sources(i + 1)
                if exists(i - 2):
                    tile_sums(i - 2)
                if exists(i + 1):
                    keys_by_block(i + 1)
                if exists(i):
                    attention_blocks(i)
                if exists(i + 1):
                    values(i + 1)

            act.wait_ge(blocks_zero, 2)
            act.wait_ge(loaded, 16 * LOADS)
            turned_targets(0)
            turned_sources(0)
            keys_by_block(0)
            values(0)
            for i in range(2):
                body(i)
            with act.Fori(2, NB - 1) as i:
                body(i)
            for i in range(NB - 1, NB + 2):
                body(i)

            node_pass(second)

            def rel_turned(b, u):
                act.wait_ge(rT_psum, b + 1)
                if is_past(b, 2):
                    act.wait_ge(y_psum, J * (b - 1))
                nc.scalar.copy(r_T[u][:], ps_d[:]).then_inc(rT_ready, 1)

            def rel_sums(b, u):
                act.wait_ge(sum2_psum, b + 1)
                if is_past(b, 2):
                    for t in range(2):
                        act.wait_ge(added2[t], 8 * J * (b - 1))
                nc.scalar.copy(r_sum[u][:].rearrange("p j d -> p (j d)"), ps_c[:, 0:512]).then_inc(sum2, 1)

            def rel_mask(b, u, j):
                act.wait_ge(y_psum, J * b + j + 1)
                act.wait_ge(hot2, b + 1)
                if is_past(b, 1):
                    act.wait_ge(selected, J * (b - 1) + j + 1)
                by_rel = r_picked[j][:].rearrange("p (o r) -> p r o", r=R)
                for q in range(0 if j % 2 == 1 else R // 2, R):
                    last = nc.scalar.activation(by_rel[:, q], (ps_a, ps_b)[j % 2][:, D * q:D * (q + 1)], ACT.Copy,
                                                scale=hot[u][:, j, q:q + 1])
                last.then_inc((masked_even_b, masked_odd)[j % 2], 1)

            def rel_body(b, u):
                if exists(b):
                    for j in range(3):
                        rel_mask(b, u, j)
                if exists(b + 1):
                    rel_turned(b + 1, 1 - u)
                if exists(b - 1):
                    rel_sums(b - 1, 1 - u)
                if exists(b):
                    rel_mask(b, u, 3)

            rel_turned(0, 0)
            for u in range(2):
                rel_body(u, u)
            with act.Fori(2, NB - 3, 2) as b:
                for u in range(2):
                    rel_body(b + u, u)
            for b in range(NB - 2, NB + 1):
                rel_body(b, b % 2)

            def last_body(n, u):
                v = u % 2
                if exists(n - 2, NN):
                    act.wait_ge(nT_psum, n - 1)
                    if is_past(n, 4):
                        act.wait_ge(nself_psum, n - 3)
                    nc.scalar.copy(n_T[v][:, 0:NT * P], n_T_ps(v)).then_inc(nT_ready, 1)
                if exists(n, NN):
                    if is_past(n, 2):
                        act.wait_ge(nT_psum, n - 1)
                    normalise(third, n, u, l_h[v])

            for n in range(8):
                last_body(n, n)
            with act.Fori(8, NN - 7, 8) as n:
                for u in range(8):
                    last_body(n + u, u)
            for n in range(NN, NN + 2):
                last_body(n, n % 8)

        @block.tensor
        def _(pe):
            pe.wait_ge(loaded, 16 * LOADS)
            pe.wait_ge(const_ready, 1)
            for a in range(2):
                last = nc.tensor.matmul(ps_d[0:TR, 0:D], emb[:, a, :], wo[:, a, :], start=(a == 0), stop=(a == 1))
            last.then_inc(type_psum, 1)
            pe.wait_ge(prep, PREP_STEPS)

            def turn_targets(b):
                pe.wait_ge(gathered_d, 16 * J * (b + 1))
                if is_past(b, 1):
                    pe.wait_ge(hTd_ready, b)
                for j in range(J):
                    last = nc.tensor.transpose(ps_e[:, P * j:P * (j + 1)], hg[:, J + j, :], ident[:])
                last.then_inc(hT_psum_d, 1)

            def turn_sources(b):
                pe.wait_ge(gathered_s, 16 * J * (b + 1))
                if is_past(b, 3):
                    pe.wait_ge(o_ready, b - 2)
                elif is_past(b, 1):
                    pe.wait_ge(hTs_ready, b)
                for j in range(J):
                    last = nc.tensor.transpose(ps_d[:, P * j:P * (j + 1)], hg[:, j, :], ident[:])
                last.then_inc(hT_psum_s, 1)

            def projection(dest, w, cols, done=None, halves=(0, 1), bias=None):
                for half in halves:
                    bank = slice(512 * half, 512 * (half + 1))
                    if bias is not None:
                        nc.tensor.matmul(dest[:, bank], bias[:, 0, P * half:P * (half + 1)],
                                         head_cols[:].rearrange("p h c -> p (h c)"), start=True, stop=False)
                    for h in range(4 * half, 4 * half + 4):
                        for s in range(4):
                            last = nc.tensor.matmul(dest[DH * s:DH * (s + 1), P * h:P * (h + 1)],
                                                    w[:, DH * h:DH * (h + 1)], cols(s), start=(bias is None),
                                                    stop=(bias is None or h % 4 == 3))
                if done is not None:
                    last.then_inc(done, 1)

            def keys(b, half):
                pe.wait_ge(hTd_ready, b + 1)
                if is_past(b, 2):
                    pe.wait_ge(m_ready, 2 * b - 3 + half)
                projection(ps_b, wk, lambda j: hTd[:, P * j:P * (j + 1)], (None, k_psum)[half], (half,), b_rows)

            def queries(b):
                pe.wait_ge(hTs_ready, b + 1)
                if is_past(b, 1):
                    pe.wait_ge(v_ready, b)
                projection(ps_c, wq, lambda j: hTs[:, P * j:P * (j + 1)], q_psum)

            def values(b):
                turned = hTd[:].rearrange("d (j n c e) -> d c n j e", j=J, c=4, e=EG)
                pe.wait_ge(q_ready, 2 * b + 1)
                projection(ps_c, wv, lambda c: turned[:, c], halves=(0,))
                pe.wait_ge(q_ready, 2 * b + 2)
                projection(ps_c, wv, lambda c: turned[:, c], v_psum, halves=(1,))

            def scores(b):
                before, = counts(pe, b - 1)
                all_k, all_q = counts(pe, J * (b + 1), 2 * (b + 1))
                pe.wait_ge(const_ready, 1)
                pe.wait_ge(k_ready, all_k)
                pe.wait_ge(q_ready, all_q)
                if is_past(b, 2):
                    pe.wait_ge(hot_ready, before)
                for g in range(G):
                    c = g % 4
                    last = nc.tensor.matmul(ps_a[TOK * c:TOK * (c + 1), P * (g // 4):P * (g // 4 + 1)],
                                            q_tok[:, TOK * g:TOK * (g + 1)],
                                            k_blk[:, g].rearrange("p j t -> p (j t)"), start=True, stop=True)
                last.then_inc(s_psum, 1)

            def messages(b):
                turned_all, now = counts(pe, 4 * (b + 1), b + 1)
                pe.wait_ge(const_ready, 1)
                pe.wait_ge(a_blocked, turned_all)
                pe.wait_ge(vT_ready, now)
                for n in range(G):
                    g8, j = n // J, n % J
                    last = nc.tensor.matmul(ps_b[DH * j:DH * (j + 1), P * g8:P * (g8 + 1)],
                                            vT[:, TOK * n:TOK * (n + 1)],
                                            a_blk[:, n].rearrange("p c t -> p (c t)"), start=True, stop=True)
                last.then_inc(m_psum, 1)

            def key_rows(dest, parts, j):
                for k in range(2):
                    last = nc.tensor.matmul(dest, parts[:, J * k + j:J * k + j + 1].to_broadcast([P, P]), ident_b[:],
                                            start=(k == 0), stop=(k == 1))
                return last

            def rows(b):
                pe.wait_ge(parts_ready, b + 1)
                if exists(b + 1):
                    pe.wait_ge(soft, 8 * (b + 1) + 1)
                if is_past(b, 1):
                    pe.wait_ge(sum_ready, b)
                for j in range(J):
                    key_rows(ps_a[:, P * j:P * (j + 1)], edge_p, j)
                    last = nc.tensor.matmul(ps_a[:, 512 + P * j:512 + P * (j + 1)],
                                            edge_p[:, 2 * J + j:2 * J + j + 1].to_broadcast([P, P]), ident_b[:],
                                            start=True, stop=True)
                last.then_inc(rows_psum, 1)

            def edge_out(b):
                pe.wait_ge(m_moved, 256 * (b + 1))
                pe.wait_ge(hot_ready, b + 1)
                if exists(b + 2):
                    pe.wait_ge(hTs_ready, b + 3)
                else:
                    pe.wait_ge(o_ready, b)
                for j in range(J):
                    o = ps_d[:, P * j:P * (j + 1)]
                    nc.tensor.matmul(o, m_dense[:, 0, j, :], wo[:, 0, :], start=True, stop=False)
                    nc.tensor.matmul(o, m_dense[:, 1, j, :], wo[:, 1, :], start=False, stop=False)
                    last = nc.tensor.matmul(o, type_hot[:, P * j:P * (j + 1)], type_out[:, 0],
                                            start=False, stop=True)
                last.then_inc(o_psum, 1)

            def tile_sums(b):
                pe.wait_ge(o_ready, b + 1)
                pe.wait_ge(same_ready, b + 1)
                if exists(b + 2):
                    pe.wait_ge(soft, 8 * (b + 2) + 1)
                else:
                    pe.wait_ge(hot_ready, b + 1)
                for j in range(J):
                    last = nc.tensor.matmul(ps_a[:, P * j:P * (j + 1)], same[:, j, :], out_e[:, j, :],
                                            start=True, stop=True)
                last.then_inc(sum_psum, 1)

            def body(i):
                if exists(i):
                    scores(i)
                if exists(i + 1):
                    turn_targets(i + 1)
                if exists(i - 1):
                    messages(i - 1)
                if exists(i - 2):
                    edge_out(i - 2)
                if exists(i + 1):
                    keys(i + 1, 0)
                    turn_sources(i + 1)
                if exists(i - 2):
                    tile_sums(i - 2)
                if exists(i + 1):
                    keys(i + 1, 1)
                    queries(i + 1)
                if exists(i - 1):
                    rows(i - 1)
                if exists(i + 1):
                    values(i + 1)

            turn_targets(0)
            keys(0, 0)
            turn_sources(0)
            keys(0, 1)
            queries(0)
            values(0)
            for i in range(2):
                body(i)
            with pe.Fori(2, NB - 1) as i:
                body(i)
            for i in range(NB - 1, NB + 2):
                body(i)

            def rel_turn(b, u):
                pe.wait_ge(gathered2[u], 16 * J * (b // 2 + 1) if isinstance(b, int) else b * 32 + 64 - 32 * u)
                if is_past(b, 1):
                    pe.wait_ge(rT_ready, b)
                for j in range(J):
                    last = nc.tensor.transpose(ps_d[:, P * j:P * (j + 1)], hg[:, J * u + j, :], ident[:])
                last.then_inc(rT_psum, 1)

            def rel_rows(b, u):
                pe.wait_ge(parts2, b + 1)
                if is_past(b, 1):
                    pe.wait_ge(same2, b)
                for j in range(J):
                    last = key_rows(ps_e[:, P * j:P * (j + 1)], r_parts[u], j)
                last.then_inc(rows2_psum, 1)

            def rel_product(b, u, j):
                if j == 0:
                    pe.wait_ge(rT_ready, b + 1)
                if is_past(b, 1) or j >= 2:
                    pe.wait_ge((masked_even, masked_odd)[j % 2], J // 2 * b + j // 2)
                    if j % 2 == 0:
                        pe.wait_ge(masked_even_b, J // 2 * b + j // 2)
                y = (ps_a, ps_b)[j % 2]
                for a in range(2):
                    last = nc.tensor.matmul(y[:, 512 * a:512 * (a + 1)], r_T[u][:, P * j:P * (j + 1)],
                                            w_rel[:, 4 * a:4 * (a + 1), :].rearrange("p r o -> p (r o)"),
                                            start=True, stop=True)
                last.then_inc(y_psum, 1)

            def rel_sums(b, u):
                pe.wait_ge(selected, J * (b + 1))
                pe.wait_ge(same2, b + 1)
                if is_past(b, 1):
                    pe.wait_ge(sum2, b)
                for j in range(J):
                    last = nc.tensor.matmul(ps_c[:, P * j:P * (j + 1)], r_same[u][:, j, :], r_sel[u][:, j, :],
                                            start=True, stop=True)
                last.then_inc(sum2_psum, 1)

            def rel_body(b, u):
                if exists(b):
                    rel_product(b, u, 0)
                    rel_product(b, u, 1)
                    rel_product(b, u, 2)
                if exists(b + 1):
                    rel_turn(b + 1, 1 - u)
                if exists(b - 1):
                    rel_sums(b - 1, 1 - u)
                if exists(b):
                    rel_product(b, u, 3)
                if exists(b + 1):
                    rel_rows(b + 1, 1 - u)

            rel_rows(0, 0)
            rel_turn(0, 0)
            for u in range(2):
                rel_body(u, u)
            with pe.Fori(2, NB - 3, 2) as b:
                for u in range(2):
                    rel_body(b + u, u)
            for b in range(NB - 2, NB + 1):
                rel_body(b, b % 2)

            def last_body(n, u):
                v = u % 2
                if exists(n - 2, NN):
                    pe.wait_ge(nT_ready, n - 1)
                    if is_past(n, 4):
                        pe.wait_ge(self_added, n - 3)
                    for k in range(NT):
                        last = nc.tensor.matmul(n_self_ps(v)[:, k, :], n_T[v][:, P * k:P * (k + 1)], w_self[:],
                                                start=True, stop=True)
                    last.then_inc(nself_psum, 1)
                if exists(n, NN):
                    pe.wait_ge(third.h, NT * (n + 1))
                    for k in range(NT):
                        last = nc.tensor.transpose(n_T_ps(v)[:, P * k:P * (k + 1)], l_h[v][:, k, :], ident[:])
                    last.then_inc(nT_psum, 1)

            for n in range(4):
                last_body(n, n)
            with pe.Fori(4, NN - 3, 4) as n:
                for u in range(4):
                    last_body(n + u, u)
            for n in range(NN, NN + 2):
                last_body(n, n % 4)


def kernel(**inputs):
    import numpy as np
    import concourse.bacc as bacc
    from concourse import mybir as mb
    from concourse.bass_utils import run_bass_kernel_spmd

    def turned(name):
        return np.ascontiguousarray(np.asarray(inputs[name]).T)

    def by_head(name):
        b = np.asarray(inputs[name]).reshape(2, 4, DH)
        return np.ascontiguousarray(np.tile(np.tile(b, (1, 1, 4)).transpose(1, 0, 2).reshape(4, 2 * P), (SPLIT, 1)))

    def by_feature(name):
        return np.ascontiguousarray(np.tile(np.asarray(inputs[name]).reshape(H, DH).T, (4, 1)))

    def plain(name):
        return np.ascontiguousarray(inputs[name])

    given = {
        "x": plain("x"), "src": plain("src"), "dst": plain("dst"),
        "et3": plain("edge_type_3"), "et8": plain("edge_type_8"),
        "wqT": turned("L0_gnn_Wq"), "bqC": by_feature("L0_gnn_bq"),
        "wkT": turned("L0_gnn_Wk"), "bkR": by_head("L0_gnn_bk"),
        "wvT": turned("L0_gnn_Wv"), "bvC": by_feature("L0_gnn_bv"),
        "embT": np.ascontiguousarray(np.tile(turned("L0_gnn_edge_emb"), (1, SPLIT))),
        "woT": turned("L0_gnn_Wo"), "bo": plain("L0_gnn_bo"),
        "wrel": plain("L1_gnn_weight"), "wself": plain("L1_gnn_self_loop_weight"), "bias1": plain("L1_gnn_bias"),
    }
    nc = bacc.Bacc("TRN2", target_bir_lowering=False, num_devices=1)
    aps = {k: nc.dram_tensor(f"in_{k}", a.shape, mb.dt.from_np(a.dtype), kind="ExternalInput").ap()
           for k, a in given.items()}
    out = nc.dram_tensor("out", (N, D), mb.dt.float32, kind="ExternalOutput").ap()
    build(nc, *aps.values(), out)
    r = run_bass_kernel_spmd(nc, [{f"in_{k}": a for k, a in given.items()}], core_ids=[0])
    return r.results[0]["out"]
```
